# Optimizing a Trainium2 kernel written in Bass

```python
import numpy as np
import jax
import jax.numpy as jnp

def _softmax(x, axis=-1):
    return jax.nn.softmax(x, axis=axis)

def _gelu(x):
    return jax.nn.gelu(x, approximate=True)

def _silu(x):
    return jax.nn.silu(x)

def _sigmoid(x):
    return jax.nn.sigmoid(x)

def _layernorm(x, axis=-1, eps=1e-05):
    m = jnp.mean(x, axis=axis, keepdims=True)
    v = jnp.var(x, axis=axis, keepdims=True)
    return (x - m) / jnp.sqrt(v + eps)

def _scatter_add(tgt, idx, src, axis=0):
    return tgt.at[idx].add(src)

def _segment_sum(src, seg, n):
    return jax.ops.segment_sum(src, seg, n)
kernel_name = 'mk_recurrent_d1_jaxref_r4_dee1c3'

def setup_inputs(seed: int=0):
    np.random.seed(seed)
    _w = jnp.asarray

    def _L0_attn_setup():
        import jax, jax.numpy as jnp
        import numpy as np
        B, S, H = (4, 512, 512)
        key = jax.random.key(seed)
        k1, k2, k3 = jax.random.split(key, 3)
        xav_qkv = float(np.sqrt(6.0 / (H + 3 * H)))
        xav_out = float(np.sqrt(6.0 / (H + H)))
        return {'hidden_states': jax.random.normal(k1, (B, S, H), dtype=jnp.float32), 'w_qkv': jax.random.uniform(k2, (3 * H, H), minval=-xav_qkv, maxval=xav_qkv, dtype=jnp.float32), 'b_qkv': jnp.zeros((3 * H,), dtype=jnp.float32), 'w_out': jax.random.uniform(k3, (H, H), minval=-xav_out, maxval=xav_out, dtype=jnp.float32), 'b_out': jnp.zeros((H,), dtype=jnp.float32)}
    _L0_attn_in = _L0_attn_setup()

    def _L0_ffn_setup():
        import jax, jax.numpy as jnp
        import numpy as np
        TOP_K = 2
        EPS = 1e-06
        key = jax.random.key(seed)
        ks = jax.random.split(key, 5)
        B, S, D, E = (4, 512, 512, 8)
        sd = 1.0 / np.sqrt(D)
        return {'x': jax.random.normal(ks[0], (B, S, D), jnp.float32), 'router_w': jax.random.normal(ks[1], (D, E), jnp.float32) * sd, 'router_b': jnp.zeros((E,), jnp.float32), 'expert_w': jax.random.normal(ks[2], (E, D, D), jnp.float32) * sd, 'expert_b': jnp.zeros((E, D), jnp.float32), 'proj_w': jax.random.normal(ks[3], (D, D), jnp.float32) * sd, 'proj_b': jnp.zeros((D,), jnp.float32), 'norm_w': jnp.ones((D,), jnp.float32)}
    _L0_ffn_in = _L0_ffn_setup()
    _d = {'L0_attn_hidden_states': _L0_attn_in['hidden_states'], 'L0_attn_w_qkv': _L0_attn_in['w_qkv'], 'L0_attn_b_qkv': _L0_attn_in['b_qkv'], 'L0_attn_w_out': _L0_attn_in['w_out'], 'L0_attn_b_out': _L0_attn_in['b_out'], 'L0_ffn_router_w': _L0_ffn_in['router_w'], 'L0_ffn_router_b': _L0_ffn_in['router_b'], 'L0_ffn_expert_w': _L0_ffn_in['expert_w'], 'L0_ffn_expert_b': _L0_ffn_in['expert_b'], 'L0_ffn_proj_w': _L0_ffn_in['proj_w'], 'L0_ffn_proj_b': _L0_ffn_in['proj_b'], 'L0_ffn_norm_w': _L0_ffn_in['norm_w']}
    _x0 = _d['L0_attn_hidden_states']
    _d['L0_attn_hidden_states'] = jax.random.normal(jax.random.fold_in(jax.random.key(seed), 1), (2, 1024, 512), dtype=_x0.dtype)
    del _x0
    return _d

def reference(L0_attn_hidden_states, L0_attn_w_qkv, L0_attn_b_qkv, L0_attn_w_out, L0_attn_b_out, L0_ffn_router_w, L0_ffn_router_b, L0_ffn_expert_w, L0_ffn_expert_b, L0_ffn_proj_w, L0_ffn_proj_b, L0_ffn_norm_w):

    def _L0_attn_ref(hidden_states, w_qkv, b_qkv, w_out, b_out):
        import jax, jax.numpy as jnp
        import numpy as np
        B, S, H = (4, 512, 512)
        Bc, Sc, Hc = hidden_states.shape
        scaling = jnp.sqrt(jnp.asarray(Hc, hidden_states.dtype))
        qkv = jnp.einsum('bsh,oh->bso', hidden_states, w_qkv) + b_qkv
        q, k, v = jnp.split(qkv, 3, axis=-1)
        scores = jnp.einsum('bqh,bkh->bqk', q, k) / scaling
        probs = jax.nn.softmax(scores, axis=-1)
        context = jnp.einsum('bqk,bkh->bqh', probs, v)
        out = jnp.einsum('bsh,oh->bso', context, w_out) + b_out
        return out

    def _L0_ffn_ref(x, router_w, router_b, expert_w, expert_b, proj_w, proj_b, norm_w):
        import jax, jax.numpy as jnp
        import numpy as np
        TOP_K = 2
        EPS = 1e-06
        B, S, D = x.shape
        E = router_b.shape[0]
        logits = jnp.einsum('bsd,de->bse', x, router_w) + router_b
        topk_vals, topk_idx = jax.lax.top_k(logits, TOP_K)
        topk_w = jax.nn.softmax(topk_vals, axis=-1)
        full_w = jnp.sum(jax.nn.one_hot(topk_idx, E, dtype=x.dtype) * topk_w[..., None], axis=-2)
        xf = x.reshape(-1, D)
        h = jnp.einsum('td,edf->etf', xf, expert_w) + expert_b[:, None, :]
        expert_out = jax.nn.silu(h)
        combined = jnp.einsum('etf,te->tf', expert_out, full_w.reshape(-1, E)).reshape(B, S, D)
        out = jnp.einsum('bsd,df->bsf', combined, proj_w) + proj_b
        y = x + out
        rms = jnp.sqrt(jnp.mean(y * y, axis=-1, keepdims=True) + EPS)
        return norm_w * (y / rms)
    x = L0_attn_hidden_states
    xn = _layernorm(x, axis=-1)
    s = _L0_attn_ref(xn, L0_attn_w_qkv, L0_attn_b_qkv, L0_attn_w_out, L0_attn_b_out)
    g = _silu(_L0_ffn_ref(xn, L0_ffn_router_w, L0_ffn_router_b, L0_ffn_expert_w, L0_ffn_expert_b, L0_ffn_proj_w, L0_ffn_proj_b, L0_ffn_norm_w))
    x = x + s * g
    return x

_drawn_inputs = setup_inputs


def setup_inputs(seed=0):
    import zlib

    import numpy as np

    out = dict(_drawn_inputs(seed))
    spreads = {'L0_attn_b_qkv': (0.0, 0.1),
     'L0_attn_b_out': (0.0, 0.1),
     'L0_ffn_router_b': (0.0, 0.446),
     'L0_ffn_expert_b': (0.0, 0.8),
     'L0_ffn_proj_b': (0.0, 0.387),
     'L0_ffn_norm_w': (1.0, 0.2)}
    factors = {}
    for name, (base, spread) in spreads.items():
        noise = np.random.default_rng([zlib.crc32(name.encode()), seed]).standard_normal(out[name].shape)
        drawn = base * np.exp(spread * noise) if base else spread * noise
        out[name] = jnp.asarray(drawn.astype(out[name].dtype))
    for name, factor in factors.items():
        out[name] = (out[name] * factor).astype(out[name].dtype)
    return out
```

```python
from contextlib import ExitStack

import concourse.bass as bass
from concourse import mybir

P = 128
F32 = mybir.dt.float32
F32R = mybir.dt.float32r
I32 = mybir.dt.int32
ALU = mybir.AluOpType
ACT = mybir.ActivationFunctionType
AX = mybir.AxisListType
ds = bass.ds

LN_EPS = 1e-5
RMS_EPS = 1e-6
RSQRT_SEED = float(0x5F3759DF)


class Chain:

    def __init__(self, eng, sem):
        self.eng, self.sem, self.base, self.k, self.total = eng, sem, 0, 0, 0

    def __call__(self, ins):
        self.k += 1
        ins.then_inc(self.sem, 1)
        self.eng.wait_ge(self.sem, self.base + self.k)

    def enter(self, turn, steps):
        self.total = self.base + self.k
        self.base, self.k, self.steps = self.total + turn * steps, 0, steps

    def leave(self, turns):
        assert self.k == self.steps, (self.k, self.steps)
        self.base, self.k = self.total + turns * self.steps, 0


def gated_attention_moe(nc, x, w_qkv, b_qkv, w_out_t, b_out, router_w, router_b,
                        expert_w, expert_b, proj_w, proj_b, norm_w, out):
    B, S, D = x.shape
    E = router_w.shape[1]
    T = B * S
    KC = D // P
    G = T // P
    GB = S // P
    QB = 4
    NB = GB // QB
    NP = E + 2
    SLOT_TILES = 2 * T // P + E
    EARLY = 3
    SCALE = float(D) ** -0.5
    assert D == KC * P == 512 and GB % QB == 0 and SLOT_TILES % 2 == 0

    x_v = x.rearrange("b (t p) h -> b p t h", p=P)
    x_g = x.rearrange("b (t p) h -> (b t) p h", p=P)
    out_g = out.rearrange("b (t p) h -> (b t) p h", p=P)
    wqkv_v = w_qkv.rearrange("(w c p) h -> w p c h", w=3, p=P)
    wout_v = w_out_t.rearrange("(c p) n -> p c n", p=P)
    expert_v = expert_w.rearrange("e (c p) f -> e p c f", p=P)
    proj_v = proj_w.rearrange("(c p) f -> p c f", p=P)

    xn_d = nc.dram_tensor("xn_scratch", (T, D), F32).ap()
    s_d = nc.dram_tensor("s_scratch", (T, D), F32).ap()
    y_d = nc.dram_tensor("y_scratch", (SLOT_TILES * P, D), F32).ap()
    tab_d = nc.dram_tensor("slot_token", (SLOT_TILES * P, 1), I32).ap()
    xn_g = xn_d.rearrange("(g p) h -> g p h", p=P)
    s_g = s_d.rearrange("(g p) h -> g p h", p=P)
    y_g = y_d.rearrange("(g p) h -> g p h", p=P)
    tab_g = tab_d.rearrange("(g p) h -> g p h", p=P)

    with ExitStack() as ctx:
        def sb(name, shape, dt=F32, stack=ctx):
            return stack.enter_context(nc.sbuf_tensor(name, shape, dt))

        def sem(name):
            return ctx.enter_context(nc.semaphore(name))

        def sems(name, n):
            return [sem(f"{name}{i}") for i in range(n)]

        ident = sb("ident", [P, P])
        ones = sb("ones", [P, P])
        tri = sb("tri", [P, P])
        rank8 = sb("rank8", [P, G, E])
        thr = sb("thr", [P, E, G])
        slot_i = sb("slot_i", [P, SLOT_TILES, E])
        ids = sb("ids", [P, G], I32)
        logits = sb("logits", [P, G, NP])
        bcols = sb("bcols", [P, 3, KC])
        tb = sb("tb", [P, KC])
        stats = sb("stats", [P, GB, 6])
        mean = sb("mean", [P, G])
        rstd = sb("rstd", [P, G])
        shift = sb("shift", [P, G])
        small = sb("small", [P, 12, 16])
        rw = sb("rw", [P, KC, NP])
        rw_h = sb("rw_h", [P, KC, NP], F32R)
        rw_l = sb("rw_l", [P, KC, NP], F32R)
        rb_bc = sb("rb_bc", [P, NP])
        sbias = sb("sbias", [P, D])
        w1 = sb("w1", [P, G])
        w2 = sb("w2", [P, G])
        pos1 = sb("pos1", [P, G], I32)
        pos2 = sb("pos2", [P, G], I32)
        texp = sb("texp", [P, SLOT_TILES], I32)
        idx = sb("idx", [P, 8], I32)
        zeros = sb("zeros", [P, SLOT_TILES], I32)
        idv = sb("idv", [P, 1], I32)
        st_h = sb("st_h", [P, 2, KC, P], F32R)
        st_l = sb("st_l", [P, 2, KC, P], F32R)
        xb = sb("xb", [P, GB, D])
        wraw = xb[:, :, :].rearrange("p (a c) n -> p a c n", a=2)
        xn = sb("xn", [P, 2, D])

        with ExitStack() as a:
            wkeep = sb("wkeep", [P, EARLY - 1, 2, KC, D], F32R, a)
            nw_h = sb("nw_h", [P, KC, D], F32R, a)
            nw_l = sb("nw_l", [P, KC, D], F32R, a)
            xt_h = sb("xt_h", [P, KC, S], F32R, a)
            xt_l = sb("xt_l", [P, KC, S], F32R, a)
            v_h = sb("v_h", [P, GB, D], F32R, a)
            v_l = sb("v_l", [P, GB, D], F32R, a)
            mw_h = sb("mw_h", [P, KC, D], F32R, a)
            mw_l = sb("mw_l", [P, KC, D], F32R, a)
            t_h = sb("t_h", [P, KC, QB * P], F32R, a)
            t_l = sb("t_l", [P, KC, QB * P], F32R, a)
            pt_h = sb("pt_h", [P, 2, GB, P], F32R, a)
            pt_l = sb("pt_l", [P, 2, GB, P], F32R, a)
            prob = sb("prob", [P, S], F32, a)
            so = sb("so", [P, 2, D], F32, a)
        with ExitStack() as a:
            raw = [sb(f"raw_{n}", [P, KC, D], F32, a) for n in ("q", "k", "v", "o")]
        with ExitStack() as a:
            W = sb("W", [P, E, 2, KC, D], F32R, a)
            bias_e = sb("bias_e", [P, E, D], F32, a)
            pw_h = sb("pw_h", [P, KC, D], F32R, a)
            pw_l = sb("pw_l", [P, KC, D], F32R, a)
            xg = sb("xg", [P, 2, D], F32, a)
            yt = sb("yt", [P, 2, D], F32, a)
        with ExitStack() as a:
            R = 4
            xf = sb("xf", [P, R, D], F32, a)
            sf = sb("sf", [P, R, D], F32, a)
            y1 = sb("y1", [P, R, D], F32, a)
            y2 = sb("y2", [P, R, D], F32, a)
            comb = sb("comb", [P, R, D], F32, a)
            xp = sb("xp", [P, R, D], F32, a)
            yy = sb("yy", [P, R, D], F32, a)
            z = sb("z", [P, R, D], F32, a)
            pb_bc = sb("pb_bc", [P, D], F32, a)
            nrm_bc = sb("nrm_bc", [P, D], F32, a)
            sq = sb("sq", [P, 2, D], F32, a)
        bvb = prob[:, 0:KC * P].rearrange("p (c n) -> p c n", c=KC)
        bo_bc = so[:, 0, :]
        prod = so[:, 1, 0:KC]
        with ExitStack() as a:
            route = sb("route", [P, 10, G, E], F32, a)
            padded = sb("padded", [P, 2, 2 * G, E], F32, a)
            starts = sb("starts", [P, 2, 2 * E], F32, a)
            slots = sb("slots", [P, SLOT_TILES, E], F32, a)

        sc = ctx.enter_context(nc.psum_tensor("sc", [P, 2, 2, 512], F32))
        tp = ctx.enter_context(nc.psum_tensor("tp", [P, 2, KC, P], F32))
        ab = ctx.enter_context(nc.psum_tensor("ab", [P, 2, D], F32))

        w_in = sems("w_in", 4)
        vec_in = sem("vec_in")
        x_in = sem("x_in")
        const = sem("const")
        zero_out = sem("zero_out")
        fold = sem("fold")
        fold_h = sem("fold_h")
        fold_l = sem("fold_l")
        pre = sem("pre")
        vecs = sem("vecs")
        pre_done = sem("pre_done")
        dv = sem("dv")
        xn_ready = sem("xn_ready")
        xn_st = sems("xn_st", 2)
        t_done = sem("t_done")
        hi_done = sem("hi_done")
        lo_done = sem("lo_done")
        copied = sem("copied")
        rt_done = sem("rt_done")
        lg_read = sem("lg_read")
        ab_full = sem("ab_full")
        ab_hi = sem("ab_hi")
        ab_read = sem("ab_read")
        s_done = sem("s_done")
        mx = sem("mx")
        exp_done = sem("exp_done")
        ptr_done = sem("ptr_done")
        pt_hi = sem("pt_hi")
        pt_lo = sem("pt_lo")
        so_st = sems("so_st", 2)
        a_done = sem("a_done")
        cnt = sem("cnt")
        gate_d = sem("gate_d")
        gate_e = sem("gate_e")
        routed = sem("routed")
        pl = sem("pl")
        scat = sem("scat")
        we_in = sems("we_in", 2)
        wr_in = sems("wr_in", 2)
        w_split = sem("w_split")
        w_hi = sem("w_hi")
        w_lo = sem("w_lo")
        be_in = sem("be_in")
        ix_in = sems("ix_in", 2)
        xg_in = sems("xg_in", 2)
        g_t = sem("g_t")
        g_hi = sem("g_hi")
        g_lo = sem("g_lo")
        silu_d = sem("silu_d")
        y_st = sems("y_st", 2)
        fin_in = sems("fin_in", 4)
        vec2_in = sem("vec2_in")
        y_in = sems("y_in", 4)
        c_done = sem("c_done")
        c_t = sem("c_t")
        c_hi = sem("c_hi")
        c_lo = sem("c_lo")
        xp_in = sem("xp_in")
        xp_done = sem("xp_done")
        sq_d = sem("sq_d")
        z_done = sem("z_done")
        g_done = sem("g_done")
        m_done = sem("m_done")
        o_done = sem("o_done")
        o_st = sems("o_st", 4)
        cnt_read = sem("cnt_read")

        block = ctx.enter_context(nc.Block())
        LATE = E - EARLY + 1
        PEEL = E

        @block.sync
        def _(sp):
            sp.sem_inc(so_st[0], 16)
            sp.sem_inc(so_st[1], 16)
            for q in range(R):
                sp.sem_inc(o_st[q], 16)
            sp.dma_start(xb[:, :, :], x_v[0]).then_inc(x_in, 16)
            for n in range(4):
                sp.dma_start(raw[n][:, :, :], wqkv_v[n] if n < 3 else wout_v).then_inc(w_in[n], 16)
            for b in range(B):
                with sp.Fori(0, GB // 2) as i:
                    for h in range(2):
                        sp.wait_ge(xn_ready, GB * b + 2 * i + h + 1)
                        sp.dma_start(xn_g[ds(GB * b + 2 * i + h, 1), :, :].rearrange("a p n -> p (a n)"),
                                     xn[:, h, :]).then_inc(xn_st[h], 16)
                if b + 1 < B:
                    sp.dma_start(xb[:, :, :], x_v[b + 1]).then_inc(x_in, 16)
                with sp.Fori(0, NB) as i:
                    for j in range(QB):
                        sp.wait_ge(ab_read, 2 + 24 * b + 8 + 8 * i + 4 + j + 1)
                        sp.dma_start(s_g[ds(GB * b + QB * i + j, 1), :, :].rearrange("a p n -> p (a n)"),
                                     so[:, j % 2, :]).then_inc(so_st[j % 2], 16)

            def load_late(n):
                e = EARLY + n
                if n < 2:
                    sp.wait_ge(w_split, 2 * (e - 1))
                else:
                    sp.wait_ge(w_lo, n - 1)
                sp.dma_start(wraw[:, e % 2, :, :], expert_v[e] if e < E else proj_v)\
                    .then_inc(wr_in[e % 2], 16)

            def load_index(i, h):
                sp.dma_start(idx[:, h:h + 1], tab_g[ds(i, 1), :, :].rearrange("a p n -> p (a n)"))\
                    .then_inc(ix_in[h], 16)

            def store_y(i, h):
                sp.wait_ge(silu_d, i + 1)
                sp.dma_start(y_g[ds(i, 1), :, :].rearrange("a p n -> p (a n)"), yt[:, h, :])\
                    .then_inc(y_st[h], 16)

            def expert_step(i, j, h):
                sp.wait_ge(xg_in[h], 16 * j)
                load_index(i + 2, h)
                store_y(i, h)

            sp.wait_ge(s_done, G)
            sp.dma_start(bias_e[:, :, :].rearrange("p e f -> p (e f)"),
                         expert_b.rearrange("e f -> (e f)").rearrange("(a n) -> a n", a=1)
                         .to_broadcast([P, E * D])).then_inc(be_in, 16)
            load_late(0)
            load_late(1)
            sp.wait_ge(scat, 32 * G)
            load_index(0, 0)
            load_index(1, 1)
            for i in range(PEEL):
                if i + 2 < LATE:
                    load_late(i + 2)
                expert_step(i, i // 2 + 1, i % 2)
            with sp.Fori(PEEL // 2, SLOT_TILES // 2 - 1) as i:
                for h in range(2):
                    expert_step(2 * i + h, i + 1, h)
            for h in range(2):
                store_y(SLOT_TILES - 2 + h, h)

            sp.wait_ge(ab_full, 24 * B + SLOT_TILES)
            sp.dma_start(pb_bc[:, :], proj_b.rearrange("(a n) -> a n", a=1).to_broadcast([P, D]))\
                .then_inc(vec2_in, 16)
            sp.dma_start(nrm_bc[:, :], norm_w.rearrange("(a n) -> a n", a=1).to_broadcast([P, D]))\
                .then_inc(vec2_in, 16)
            for q in range(2):
                sp.wait_ge(so_st[q], 16 + 8 * G)

            def load_fin(g, q):
                sp.dma_start(xf[:, q, :], x_g[ds(g, 1), :, :].rearrange("a p n -> p (a n)"))\
                    .then_inc(fin_in[q], 16)
                sp.dma_start(sf[:, q, :], s_g[ds(g, 1), :, :].rearrange("a p n -> p (a n)"))\
                    .then_inc(fin_in[q], 16)

            def store_out(g, q):
                sp.wait_ge(o_done, g + 1)
                sp.dma_start(out_g[ds(g, 1), :, :].rearrange("a p n -> p (a n)"), z[:, q, :])\
                    .then_inc(o_st[q], 16)

            for q in range(R):
                load_fin(q, q)
            with sp.Fori(0, G // R - 1) as i:
                for q in range(R):
                    store_out(R * i + q, q)
                    load_fin(R * i + q + R, q)
            for q in range(R):
                store_out(G - R + q, q)
            for q in range(R):
                sp.wait_ge(o_st[q], 16 + 16 * (G // R))
            for q in range(2):
                sp.wait_ge(xn_st[q], 8 * G)
                sp.wait_ge(y_st[q], 8 * SLOT_TILES)

        @block.gpsimd
        def _(pool):
            link = Chain(pool, pl)
            pool.memset(ones[:, :], 1.0).then_inc(const, 1)
            link(pool.memset(ident[:, :], 0.0))
            pool.affine_select(out=ident[:, :], in_=ident[:, :], compare_op=ALU.not_equal, fill=1.0,
                               base=0, pattern=[[-1, P]], channel_multiplier=1).then_inc(const, 1)
            pool.wait_ge(const, 1)
            pool.affine_select(out=tri[:, :], in_=ones[:, :], compare_op=ALU.is_gt, fill=0.0,
                               base=0, pattern=[[1, P]], channel_multiplier=-1).then_inc(const, 1)
            pool.iota(rank8[:, :, :], [[0, G], [-1, E]], base=E, channel_multiplier=0,
                      allow_small_or_imprecise_dtypes=True).then_inc(const, 1)
            pool.iota(thr[:, :, :], [[0, E], [P, G]], base=0, channel_multiplier=0,
                      allow_small_or_imprecise_dtypes=True).then_inc(const, 1)
            pool.iota(slot_i[:, :, :], [[1, SLOT_TILES], [0, E]], base=0, channel_multiplier=0,
                      allow_small_or_imprecise_dtypes=True).then_inc(const, 1)
            pool.iota(ids[:, :], [[P, G]], base=0, channel_multiplier=1).then_inc(const, 1)
            link(pool.memset(zeros[:, :], 0))
            pool.dma_start(tab_d.rearrange("(p i) a -> p (i a)", p=P), zeros[:, :]).then_inc(zero_out, 16)
            pool.dma_start(bcols[:, :, :], b_qkv).then_inc(vec_in, 16)
            pool.dma_start(bo_bc, b_out.rearrange("(a n) -> a n", a=1).to_broadcast([P, D])).then_inc(vec_in, 16)
            link(pool.memset(rw[:, :, :], 0.0))
            link(pool.memset(rb_bc[:, :], 0.0))
            pool.dma_start(rw[:, :, 0:E], router_w.rearrange("(c p) e -> p c e", p=P)).then_inc(vec_in, 16)
            pool.dma_start(rb_bc[:, 0:E], router_b.rearrange("(a n) -> a n", a=1).to_broadcast([P, E]))\
                .then_inc(vec_in, 16)
            for b in range(B):
                with pool.Fori(0, GB // 2) as i:
                    for h in range(2):
                        pool.wait_ge(lo_done, GB * b + 2 * i + h + 1)
                        pool.tensor_copy(xt_h[:, :, ds((2 * i + h) * P, P)], st_h[:, h, :, :]).then_inc(copied, 1)
                        pool.tensor_copy(xt_l[:, :, ds((2 * i + h) * P, P)], st_l[:, h, :, :]).then_inc(copied, 1)
            pool.wait_ge(routed, 1)
            pool.wait_ge(zero_out, 16)
            with pool.Fori(0, G) as g:
                link.enter(g, 3)
                link(pool.tensor_copy(idx[:, 2:3], pos1[:, ds(g, 1)]))
                link(pool.tensor_copy(idx[:, 3:4], pos2[:, ds(g, 1)]))
                link(pool.tensor_copy(idv[:, :], ids[:, ds(g, 1)]))
                pool.nop(nofuse=True)
                for c in (2, 3):
                    pool.indirect_dma_start(tab_d, bass.IndirectOffsetOnAxis(idx[:, c:c + 1], 0),
                                            idv[:, :], None).then_inc(scat, 16)
                pool.wait_ge(scat, 32 * g + 32)
            link.leave(G)
            for e in range(2):
                pool.dma_start(wraw[:, e, :, :], expert_v[e]).then_inc(we_in[e % 2], 16)
            for e in range(EARLY):
                pool.wait_ge(we_in[e % 2], 16 * (e // 2 + 1))
                pool.tensor_copy(W[:, e, 0, :, :], wraw[:, e % 2, :, :]).then_inc(w_split, 1)
                pool.wait_ge(w_split, 2 * e + 1)
                pool.tensor_tensor(W[:, e, 1, :, :], wraw[:, e % 2, :, :], W[:, e, 0, :, :], ALU.subtract)\
                    .then_inc(w_split, 1)
                if e + 2 < EARLY:
                    pool.wait_ge(w_split, 2 * e + 2)
                    pool.dma_start(wraw[:, e % 2, :, :], expert_v[e + 2]).then_inc(we_in[e % 2], 16)

            def gather(h, n):
                pool.wait_ge(ix_in[h], 16 * n)
                pool.nop(nofuse=True)
                pool.indirect_dma_start(xg[:, h, :], None, xn_d,
                                        bass.IndirectOffsetOnAxis(idx[:, h:h + 1], 0)).then_inc(xg_in[h], 16)

            pool.wait_ge(ptr_done, 1 + G)
            for q in range(2):
                pool.wait_ge(xn_st[q], 8 * G)
            gather(0, 1)
            gather(1, 1)
            with pool.Fori(0, SLOT_TILES // 2 - 1) as i:
                for h in range(2):
                    pool.wait_ge(g_t, 2 * i + h + 1)
                    gather(h, i + 2)
            for q in range(2):
                pool.wait_ge(y_st[q], 8 * SLOT_TILES)

            def gather_y(g, q):
                link(pool.tensor_copy(idx[:, 2 * q:2 * q + 1], pos1[:, ds(g, 1)]))
                link(pool.tensor_copy(idx[:, 2 * q + 1:2 * q + 2], pos2[:, ds(g, 1)]))
                pool.nop(nofuse=True)
                for n, y in enumerate((y1, y2)):
                    pool.indirect_dma_start(y[:, q, :], None, y_d,
                                            bass.IndirectOffsetOnAxis(idx[:, 2 * q + n:2 * q + n + 1], 0))\
                        .then_inc(y_in[q], 16)

            def residual(g, q):
                pool.wait_ge(xp_in, g + 1)
                pool.tensor_tensor(xp[:, q, :], xp[:, q, :], pb_bc[:, :], ALU.add).then_inc(xp_done, 1)

            def add_x(g, q):
                pool.wait_ge(m_done, g + 1)
                pool.tensor_tensor(z[:, q, :], z[:, q, :], xf[:, q, :], ALU.add).then_inc(o_done, 1)

            def last_step(g, q, before=True, after=True, next_=True):
                if next_:
                    residual(g + 1, (q + 1) % R)
                if after:
                    pool.wait_ge(c_done, g + 1)
                    gather_y(g + R, q)
                if before:
                    add_x(g - 2, (q - 2) % R)

            for q in range(R):
                gather_y(q, q)
            pool.wait_ge(vec2_in, 32)
            residual(0, 0)
            for q in range(R):
                last_step(q, q, before=q >= 2)
            with pool.Fori(1, G // R - 1) as i:
                link.enter(i - 1, 2 * R)
                for q in range(R):
                    last_step(R * i + q, q)
                link.leave(G // R - 2)
            for q in range(R):
                last_step(G - R + q, q, after=False, next_=q + 1 < R)
            for q in range(2):
                add_x(G - 2 + q, R - 2 + q)

        @block.scalar
        def _(act):
            act.sem_inc(exp_done, 2)
            for n in range(2 * KC):
                act.wait_ge(fold, n + 1)
                dst = (mw_h if n < KC else nw_h)[:, n % KC, :]
                nc.scalar.copy(dst, sc[:, (n % 4) // 2, n % 2, :]).then_inc(fold_h, 1)

            for b in range(B):
                def hi(g, h, first=False):
                    act.wait_ge(t_done, g + 1)
                    if not first:
                        act.wait_ge(copied, 2 * g - 2)
                    nc.scalar.copy(st_h[:, h, :, :], tp[:, h, :, :]).then_inc(hi_done, 1)

                def v_hi(g, t, h):
                    act.wait_ge(ab_full, 24 * b + t + 1)
                    nc.scalar.copy(v_h[:, ds(t, 1), :].rearrange("p a n -> p (a n)"), ab[:, h, :]).then_inc(ab_hi, 1)

                g0 = GB * b
                hi(g0, 0, b == 0)
                hi(g0 + 1, 1, b == 0)
                with act.Fori(0, GB // 2 - 1) as i:
                    for h in range(2):
                        v_hi(g0 + 2 * i + h, 2 * i + h, h)
                        hi(g0 + 2 * i + h + 2, h)
                for h in range(2):
                    v_hi(g0 + GB - 2 + h, GB - 2 + h, h)

                if b == B - 1:
                    act.wait_ge(gate_d, 1)
                    nc.scalar.activation(small[:, 10, :], small[:, 9, :], ACT.Exp).then_inc(gate_e, 1)

                with act.Fori(0, NB) as i:
                    for c in range(KC):
                        act.wait_ge(ab_full, 24 * b + 8 + 8 * i + c + 1)
                        nc.scalar.activation(t_h[:, c, :], ab[:, c % 2, :], ACT.Identity, bias=tb[:, c:c + 1])\
                            .then_inc(ab_hi, 1)

                    def pt_split(j):
                        act.wait_ge(ptr_done, 1 + g0 + QB * i + j + 1)
                        nc.scalar.copy(pt_h[:, j % 2, :, :], tp[:, :, :, :].rearrange("p a c n -> p (a c) n"))\
                            .then_inc(pt_hi, 1)

                    for j in range(QB):
                        if j >= 1:
                            pt_split(j - 1)
                        act.wait_ge(mx, g0 + QB * i + j + 1)
                        act.wait_ge(ptr_done, g0 + QB * i + j + 1)
                        nc.scalar.activation(prob[:, :], sc[:, j % 2, :, :].rearrange("p a n -> p (a n)"), ACT.Exp,
                                             bias=small[:, 4 + j, 1:2], scale=SCALE,
                                             accum_out=small[:, 4 + j, 2:3]).then_inc(exp_done, 1)
                    pt_split(QB - 1)

            def g_split(i, h):
                act.wait_ge(g_t, i + 1)
                nc.scalar.copy(st_h[:, h, :, :], tp[:, h, :, :]).then_inc(g_hi, 1)

            def silu(i, h):
                act.wait_ge(ab_read, 2 + 24 * B + i + 1)
                nc.scalar.activation(yt[:, h, :], yt[:, h, :], ACT.Silu).then_inc(silu_d, 1)

            def w_high(n):
                e = EARLY + n
                act.wait_ge(wr_in[e % 2], 16 * (n // 2 + 1))
                dst = W[:, e, 0, :, :] if e < E else pw_h[:, :, :]
                nc.scalar.copy(dst, wraw[:, e % 2, :, :]).then_inc(w_hi, 1)

            act.wait_ge(ab_full, 24 * B)
            act.wait_ge(copied, 2 * G)
            g_split(0, 0)
            for i in range(PEEL):
                if i < LATE:
                    w_high(i)
                g_split(i + 1, (i + 1) % 2)
                silu(i, i % 2)
            with act.Fori(PEEL // 2, SLOT_TILES // 2 - 1) as i:
                for h in range(2):
                    g_split(2 * i + h + 1, 1 - h)
                    silu(2 * i + h, h)
            g_split(SLOT_TILES - 1, 1)
            silu(SLOT_TILES - 2, 0)
            silu(SLOT_TILES - 1, 1)

            def c_split(g, h):
                act.wait_ge(c_t, g + 1)
                nc.scalar.copy(st_h[:, h, :, :], tp[:, h, :, :]).then_inc(c_hi, 1)

            def squares(g, q):
                act.wait_ge(ab_read, 2 + 24 * B + SLOT_TILES + g + 1)
                nc.scalar.activation(sq[:, q % 2, :], yy[:, q, :], ACT.Square,
                                     accum_out=small[:, 0, q:q + 1]).then_inc(sq_d, 1)

            def gate(g, q):
                act.wait_ge(z_done, g + 1)
                nc.scalar.activation(z[:, q, :], z[:, q, :], ACT.Silu).then_inc(g_done, 1)

            def normalise(g, q):
                act.wait_ge(fin_in[q], 8 * (g - q) + 32)
                nc.scalar.activation(xp[:, q, :], xf[:, q, :], ACT.Identity, bias=shift[:, ds(g, 1)],
                                     scale=rstd[:, ds(g, 1)]).then_inc(xp_in, 1)

            def last_pair(g, q, more=True):
                for k in range(2):
                    if more:
                        normalise(g + k + 2, (q + k + 2) % R)
                    squares(g + k, q + k)
                    if more:
                        c_split(g + k + 2, k)
                gate(g, q)
                gate(g + 1, q + 1)

            normalise(0, 0)
            normalise(1, 1)
            c_split(0, 0)
            c_split(1, 1)
            with act.Fori(0, G // R - 1) as i:
                last_pair(R * i, 0)
                last_pair(R * i + 2, 2)
            last_pair(G - R, 0)
            last_pair(G - 2, 2, more=False)

        @block.vector
        def _(dve):
            link = Chain(dve, dv)
            vec = nc.vector

            def rsqrt(r, v, t):
                link(vec.tensor_scalar(r.bitcast(I32), v.bitcast(I32), 1, None, ALU.logical_shift_right))
                link(vec.tensor_scalar(r.bitcast(I32), r.bitcast(I32), -1.0, RSQRT_SEED, ALU.mult, ALU.add))
                for _ in range(3):
                    link(vec.tensor_tensor(t, r, r, ALU.mult))
                    link(vec.tensor_tensor(t, t, v, ALU.mult))
                    link(vec.tensor_scalar(t, t, -0.5, 1.5, ALU.mult, ALU.add))
                    link(vec.tensor_tensor(r, r, t, ALU.mult))

            dve.sem_inc(ab_read, 2)
            dve.sem_inc(pt_lo, 1)
            dve.wait_ge(vec_in, 64)
            dve.wait_ge(const, 7)
            vec.tensor_tensor(prod, bcols[:, 0, :], bcols[:, 1, :], ALU.mult).then_inc(pre, 1)
            for c in range(KC):
                vec.tensor_scalar(bvb[:, c, :], ones[:, :], bcols[:, 2, c:c + 1], None, ALU.mult).then_inc(pre, 1)

            def batch_stats(b):
                g0 = GB * b
                dve.wait_ge(x_in, 16 * (b + 1))
                with dve.Fori(0, GB) as t:
                    link.enter(t, 1)
                    link(vec.bn_stats(stats[:, ds(t, 1), :].rearrange("p a s -> p (a s)"),
                                      xb[:, ds(t, 1), :].rearrange("p a n -> p (a n)")))
                link.leave(GB)
                me, mo = stats[:, :, 1], stats[:, :, 4]
                ve, vo = stats[:, :, 2], stats[:, :, 5]
                m, r = mean[:, g0:g0 + GB], rstd[:, g0:g0 + GB]
                a, v = small[:, 0, 0:GB], small[:, 1, 0:GB]
                link(vec.tensor_tensor(a, me, mo, ALU.subtract))
                link(vec.tensor_tensor(a, a, a, ALU.mult))
                link(vec.tensor_tensor(v, ve, vo, ALU.add))
                link(vec.tensor_scalar(a, a, 0.25, LN_EPS, ALU.mult, ALU.add))
                link(vec.scalar_tensor_tensor(v, v, 1.0 / D, a, ALU.mult, ALU.add))
                link(vec.tensor_tensor(m, me, mo, ALU.add))
                link(vec.tensor_scalar(m, m, 0.5, None, ALU.mult))
                rsqrt(r, v, a)
                link(vec.scalar_tensor_tensor(shift[:, g0:g0 + GB], m, -1.0, r, ALU.mult, ALU.mult))

            def normalise(g, t, h, first=False):
                if not first:
                    dve.wait_ge(t_done, g - 1)
                    dve.wait_ge(xn_st[h], 8 * (g - h))
                vec.tensor_scalar(xn[:, h, :], xb[:, ds(t, 1), :].rearrange("p a n -> p (a n)"),
                                  mean[:, ds(g, 1)], rstd[:, ds(g, 1)], ALU.subtract, ALU.mult).then_inc(xn_ready, 1)

            def lo(g, h):
                dve.wait_ge(hi_done, g + 1)
                vec.tensor_tensor(st_l[:, h, :, :], tp[:, h, :, :], st_h[:, h, :, :], ALU.subtract).then_inc(lo_done, 1)

            def read_logits(g, h):
                dve.wait_ge(rt_done, g + 1)
                vec.tensor_tensor(logits[:, ds(g, 1), :].rearrange("p a n -> p (a n)"), sc[:, h, 0, 0:NP],
                                  rb_bc[:, :], ALU.add).then_inc(lg_read, 1)

            def v_lo(b, t, h):
                dve.wait_ge(ab_hi, 16 * b + t + 1)
                vec.tensor_tensor(v_l[:, ds(t, 1), :].rearrange("p a n -> p (a n)"), ab[:, h, :],
                                  v_h[:, ds(t, 1), :].rearrange("p a n -> p (a n)"), ALU.subtract).then_inc(ab_read, 1)

            def fold_low():
                for n in range(2 * KC):
                    dve.wait_ge(fold_h, n + 1)
                    h, l = (mw_h, mw_l) if n < KC else (nw_h, nw_l)
                    vec.tensor_tensor(l[:, n % KC, :], sc[:, (n % 4) // 2, n % 2, :], h[:, n % KC, :], ALU.subtract)\
                        .then_inc(fold_l, 1)
                dve.wait_ge(vecs, 1)
                vec.tensor_copy(tb[:, :], ab[:, 0, 0:KC]).then_inc(pre_done, 1)
                link(vec.tensor_copy(rw[:, :, E], ab[:, 0, KC:2 * KC]))
                vec.tensor_reduce(rb_bc[:, E:E + 1], ab[:, 0, 2 * KC:3 * KC], AX.X, ALU.add).then_inc(pre_done, 1)
                link(vec.tensor_tensor(sbias[:, :], ab[:, 1, :], bo_bc, ALU.add))
                link(vec.tensor_copy(rw_h[:, :, :], rw[:, :, :]))
                vec.tensor_tensor(rw_l[:, :, :], rw[:, :, :], rw_h[:, :, :], ALU.subtract).then_inc(pre_done, 1)
                dve.wait_ge(pre_done, 3)

            def choose():
                dve.wait_ge(lg_read, G)
                L = logits[:, :, 0:E]
                row = lambda n: small[:, n, :]
                wide = lambda n: route[:, n, :, :]
                per_token = lambda v: v.unsqueeze(2).to_broadcast([P, G, E])

                def best(values, top, last, onehot):
                    link(vec.tensor_reduce(top, values, AX.X, ALU.max))
                    link(vec.tensor_tensor(wide(0), values, per_token(top), ALU.is_equal))
                    link(vec.tensor_tensor(wide(0), wide(0), rank8[:, :, :], ALU.mult))
                    link(vec.tensor_reduce(last, wide(0), AX.X, ALU.max))
                    link(vec.tensor_tensor(onehot, rank8[:, :, :], per_token(last), ALU.is_equal))

                best(L, row(0), row(1), wide(1))
                link(vec.scalar_tensor_tensor(wide(2), wide(1), -3e38, L, ALU.mult, ALU.add))
                best(wide(2), row(2), row(1), wide(3))
                vec.tensor_tensor(wide(4), wide(1), wide(3), ALU.add).then_inc(a_done, 1)
                vec.tensor_tensor(row(9), row(2), row(0), ALU.subtract).then_inc(gate_d, 1)
                link(vec.memset(padded[:, :, :, :], 0.0))
                link(vec.memset(starts[:, :, :], 0.0))
                dve.wait_ge(cnt, 1)
                link(vec.tensor_copy(wide(5), sc[:, 0, 0, 0:G * E].rearrange("p (g e) -> p g e", e=E)))
                link(vec.tensor_copy(wide(6), sc[:, 1, 0, 0:G * E].rearrange("p (g e) -> p g e", e=E)))
                vec.tensor_copy(padded[:, 0, G:2 * G, :], wide(6)).then_inc(cnt_read, 1)
                dve.wait_ge(cnt_read, 1)
                dve.wait_ge(gate_e, 1)
                link(vec.tensor_scalar(row(11), row(10), 1.0, None, ALU.add))
                link(vec.reciprocal(w1[:, :], row(11)))
                link(vec.tensor_tensor(w2[:, :], w1[:, :], row(10), ALU.mult))
                src, back = 0, 1
                while back < G:
                    link(vec.tensor_tensor(padded[:, 1 - src, G:2 * G, :], padded[:, src, G:2 * G, :],
                                           padded[:, src, G - back:2 * G - back, :], ALU.add))
                    src, back = 1 - src, 2 * back
                link(vec.tensor_tensor(wide(7), padded[:, src, G:2 * G, :], wide(6), ALU.subtract))
                total = padded[:, src, 2 * G - 1, :]
                by_tile = wide(8).rearrange("p g e -> p (g e)").rearrange("p (e g) -> p e g", e=E)
                link(vec.scalar_tensor_tensor(by_tile, total.unsqueeze(2).to_broadcast([P, E, G]), 1.0, thr[:, :, :],
                                              ALU.max, ALU.is_gt))
                n_tiles, first = small[:, 8, 0:E], small[:, 11, 0:E]
                link(vec.tensor_reduce(n_tiles, by_tile, AX.X, ALU.add))
                link(vec.tensor_copy(starts[:, 0, E:2 * E], n_tiles))
                src, back = 0, 1
                while back < E:
                    link(vec.tensor_tensor(starts[:, 1 - src, E:2 * E], starts[:, src, E:2 * E],
                                           starts[:, src, E - back:2 * E - back], ALU.add))
                    src, back = 1 - src, 2 * back
                link(vec.tensor_tensor(first, starts[:, src, E:2 * E], n_tiles, ALU.subtract))
                link(vec.tensor_tensor(slots[:, :, :], slot_i[:, :, :],
                                       first.unsqueeze(1).to_broadcast([P, SLOT_TILES, E]), ALU.is_ge))
                of_tile = wide(9).rearrange("p g e -> p (g e)")[:, 0:SLOT_TILES]
                link(vec.tensor_reduce(of_tile, slots[:, :, :], AX.X, ALU.add))
                link(vec.tensor_scalar(texp[:, :], of_tile, -1.0, None, ALU.add))
                link(vec.scalar_tensor_tensor(wide(7), first.unsqueeze(1).to_broadcast([P, G, E]), float(P), wide(7),
                                              ALU.mult, ALU.add))
                link(vec.tensor_tensor(wide(7), wide(7), wide(5), ALU.add))
                for onehot, pos in ((wide(1), pos1), (wide(3), pos2)):
                    link(vec.tensor_tensor(wide(8), wide(7), onehot, ALU.mult))
                    link(vec.tensor_reduce(row(1), wide(8), AX.X, ALU.add))
                    link(vec.tensor_copy(pos[:, :], row(1)))
                dve.sem_inc(routed, 1)

            for b in range(B):
                g0 = GB * b
                batch_stats(b)
                normalise(g0, 0, 0, b == 0)
                normalise(g0 + 1, 1, 1, b == 0)
                if b == 0:
                    fold_low()
                lo(g0, 0)
                with dve.Fori(0, GB // 2 - 1) as i:
                    for h in range(2):
                        t = 2 * i + h
                        normalise(g0 + t + 2, t + 2, h)
                        lo(g0 + t + 1, 1 - h)
                        read_logits(g0 + t, h)
                        v_lo(b, t, h)
                lo(g0 + GB - 1, 1)
                for h in range(2):
                    read_logits(g0 + GB - 2 + h, h)
                    v_lo(b, GB - 2 + h, h)

                if b == B - 1:
                    choose()

                dve.wait_ge(lg_read, g0 + GB)
                with dve.Fori(0, NB) as i:
                    link.enter(i, 3 * QB)
                    for c in range(KC):
                        dve.wait_ge(ab_hi, 16 * b + 8 + KC * i + c + 1)
                        vec.scalar_tensor_tensor(t_l[:, c, :], ab[:, c % 2, :], tb[:, c:c + 1], t_h[:, c, :],
                                                 ALU.add, ALU.subtract).then_inc(ab_read, 1)

                    def row_max(j):
                        n = g0 + QB * i + j
                        key = logits[:, ds(n, 1), E:E + 1].rearrange("p a n -> p (a n)")
                        dve.wait_ge(s_done, n + 1)
                        link(vec.tensor_reduce(small[:, 4 + j, 0:1], sc[:, j % 2, :, :], AX.XY, ALU.max, negate=True))
                        link(vec.tensor_tensor(small[:, 4 + j, 1:2], small[:, 4 + j, 0:1], key, ALU.subtract))
                        vec.tensor_scalar(small[:, 4 + j, 1:2], small[:, 4 + j, 1:2], key, SCALE, ALU.add, ALU.mult)\
                            .then_inc(mx, 1)

                    def pt_low(j):
                        dve.wait_ge(pt_hi, g0 + QB * i + j + 1)
                        vec.tensor_tensor(pt_l[:, j % 2, :, :], tp[:, :, :, :].rearrange("p a c n -> p (a c) n"),
                                          pt_h[:, j % 2, :, :], ALU.subtract).then_inc(pt_lo, 1)

                    def attn_out(j):
                        dve.wait_ge(ab_full, 24 * b + 8 + 8 * i + 4 + j + 1)
                        link(vec.reciprocal(small[:, 4 + j, 3:4], small[:, 4 + j, 2:3]))
                        dve.wait_ge(so_st[j % 2], 8 * g0 + 32 * i + 16 * (j // 2) + 16)
                        vec.scalar_tensor_tensor(so[:, j % 2, :], ab[:, j % 2, :], small[:, 4 + j, 3:4], sbias[:, :],
                                                 ALU.mult, ALU.add).then_inc(ab_read, 1)

                    row_max(0)
                    row_max(1)
                    pt_low(0)
                    row_max(2)
                    pt_low(1)
                    attn_out(0)
                    row_max(3)
                    pt_low(2)
                    attn_out(1)
                    pt_low(3)
                    attn_out(2)
                    attn_out(3)
                link.leave(NB)

            def w_low(n):
                e = EARLY + n
                dve.wait_ge(w_hi, n + 1)
                hi_part, dst = (W[:, e, 0, :, :], W[:, e, 1, :, :]) if e < E else (pw_h[:, :, :], pw_l[:, :, :])
                vec.tensor_tensor(dst, wraw[:, e % 2, :, :], hi_part, ALU.subtract).then_inc(w_lo, 1)

            def g_low(i, h):
                dve.wait_ge(g_hi, i + 1)
                vec.tensor_tensor(st_l[:, h, :, :], tp[:, h, :, :], st_h[:, h, :, :], ALU.subtract).then_inc(g_lo, 1)

            def add_bias(i, h, first=False):
                e = dve.value_load(texp[0:1, ds(i, 1)], min_val=0, max_val=E - 1)
                dve.wait_ge(ab_full, 24 * B + i + 1)
                if not first:
                    dve.wait_ge(y_st[h], 8 * (i - h))
                vec.tensor_tensor(yt[:, h, :], ab[:, h, :], bias_e[:, ds(e, 1), :].rearrange("p a n -> p (a n)"),
                                  ALU.add).then_inc(ab_read, 1)

            for q in range(2):
                dve.wait_ge(so_st[q], 16 + 8 * G)
            dve.wait_ge(be_in, 16)
            g_low(0, 0)
            for i in range(PEEL):
                if i < LATE:
                    w_low(i)
                g_low(i + 1, (i + 1) % 2)
                add_bias(i, i % 2, i < 2)
            with dve.Fori(PEEL // 2, SLOT_TILES // 2 - 1) as i:
                for h in range(2):
                    g_low(2 * i + h + 1, 1 - h)
                    add_bias(2 * i + h, h)
            g_low(SLOT_TILES - 1, 1)
            add_bias(SLOT_TILES - 2, 0)
            add_bias(SLOT_TILES - 1, 1)

            def combine(g, q):
                dve.wait_ge(y_in[q], 8 * (g - q) + 32)
                link(vec.tensor_scalar(y1[:, q, :], y1[:, q, :], w1[:, ds(g, 1)], None, ALU.mult))
                vec.scalar_tensor_tensor(comb[:, q, :], y2[:, q, :], w2[:, ds(g, 1)], y1[:, q, :],
                                         ALU.mult, ALU.add).then_inc(c_done, 1)

            def c_low(g, h):
                dve.wait_ge(c_hi, g + 1)
                vec.tensor_tensor(st_l[:, h, :, :], tp[:, h, :, :], st_h[:, h, :, :], ALU.subtract).then_inc(c_lo, 1)

            def add_product(g, q):
                dve.wait_ge(xp_done, g + 1)
                dve.wait_ge(ab_full, 24 * B + SLOT_TILES + g + 1)
                vec.tensor_tensor(yy[:, q, :], ab[:, q % 2, :], xp[:, q, :], ALU.add).then_inc(ab_read, 1)

            def last_pair(g, q, more=True):
                for k in range(2):
                    if more:
                        combine(g + k + 2, (q + k + 2) % R)
                    add_product(g + k, q + k)
                    if more:
                        c_low(g + k + 2, k)
                ms, r, t = (small[:, n, q:q + 2] for n in (1, 2, 3))
                dve.wait_ge(sq_d, g + 2)
                link(vec.tensor_scalar(ms, small[:, 0, q:q + 2], 1.0 / D, RMS_EPS, ALU.mult, ALU.add))
                rsqrt(r, ms, t)
                for k in range(2):
                    dve.wait_ge(o_st[q + k], 4 * (g - q) + 16)
                    vec.scalar_tensor_tensor(z[:, q + k, :], yy[:, q + k, :], r[:, k:k + 1], nrm_bc[:, :],
                                             ALU.mult, ALU.mult).then_inc(z_done, 1)
                for k in range(2):
                    dve.wait_ge(g_done, g + k + 1)
                    vec.tensor_tensor(z[:, q + k, :], z[:, q + k, :], sf[:, q + k, :], ALU.mult).then_inc(m_done, 1)

            dve.wait_ge(vec2_in, 32)
            combine(0, 0)
            combine(1, 1)
            c_low(0, 0)
            c_low(1, 1)
            with dve.Fori(0, G // R - 1) as i:
                link.enter(i, 2 * (2 + 1 + 14))
                last_pair(R * i, 0)
                last_pair(R * i + 2, 2)
            link.leave(G // R - 1)
            last_pair(G - R, 0)
            last_pair(G - 2, 2, more=False)

        @block.tensor
        def _(pe):
            def product(dst, lh, ll, rh, rl, start, stop):
                nc.tensor.matmul(dst, lh, rh, start=start, stop=False)
                nc.tensor.matmul(dst, lh, rl, start=False, stop=False)
                return nc.tensor.matmul(dst, ll, rh, start=False, stop=stop)

            def transpose_tile(src, h):
                for c in range(KC):
                    last = nc.tensor.transpose(tp[:, h, c, :], src[:, c * P:(c + 1) * P], ident[:, :])
                return last

            pe.sem_inc(ptr_done, 1)
            for n in range(2 * KC):
                left, right = (raw[0], raw[1]) if n < KC else (raw[2], raw[3])
                if n % KC == 0:
                    for m in range(2):
                        pe.wait_ge(w_in[(n // KC) * 2 + m], 16)
                if n >= 4:
                    pe.wait_ge(fold_l, n - 3)
                for c in range(KC):
                    last = nc.tensor.matmul(sc[:, (n % 4) // 2, n % 2, :], left[:, c, (n % KC) * P:(n % KC + 1) * P],
                                            right[:, c, :], start=(c == 0), stop=(c == KC - 1))
                last.then_inc(fold, 1)
            pe.wait_ge(pre, 1 + KC)
            for m, (left, col) in enumerate(((raw[1], 0), (raw[0], 1))):
                for n in range(KC):
                    for c in range(KC):
                        nc.tensor.matmul(ab[:, 0, m * KC + n:m * KC + n + 1], left[:, c, n * P:(n + 1) * P],
                                         bcols[:, col, c:c + 1], start=(c == 0), stop=(c == KC - 1))
            nc.tensor.matmul(ab[:, 0, 2 * KC:3 * KC], ones[:, :], prod, start=True, stop=True)
            for c in range(KC):
                last = nc.tensor.matmul(ab[:, 1, :], bvb[:, c, :], raw[3][:, c, :], start=(c == 0), stop=(c == KC - 1))
            last.then_inc(vecs, 1)

            for b in range(B):
                g0 = GB * b

                def turn(g, h, first=False):
                    pe.wait_ge(xn_ready, g + 1)
                    if not first:
                        pe.wait_ge(lo_done, g - 1)
                    transpose_tile(xn[:, h, :], h).then_inc(t_done, 1)

                def tile_products(g, t, h, first=False):
                    pe.wait_ge(lo_done, g + 1)
                    if not first:
                        pe.wait_ge(lg_read, g - 1)
                    for c in range(KC):
                        last = product(sc[:, h, 0, 0:NP], st_h[:, h, c, :], st_l[:, h, c, :],
                                       rw_h[:, c, :], rw_l[:, c, :], c == 0, c == KC - 1)
                    last.then_inc(rt_done, 1)
                    pe.wait_ge(ab_read, 24 * b + t + 1)
                    for c in range(KC):
                        last = product(ab[:, h, :], st_h[:, h, c, :], st_l[:, h, c, :],
                                       nw_h[:, c, :], nw_l[:, c, :], c == 0, c == KC - 1)
                    last.then_inc(ab_full, 1)

                if b:
                    pe.wait_ge(pt_lo, 1 + g0)
                turn(g0, 0, b == 0)
                if b == 0:
                    pe.wait_ge(fold_l, 2 * KC)
                    pe.wait_ge(pre_done, 3)
                else:
                    pe.wait_ge(exp_done, 2 + g0)
                for h in range(2):
                    turn(g0 + h + 1, 1 - h, b == 0 and h == 0)
                    tile_products(g0 + h, h, h, b == 0)
                with pe.Fori(1, GB // 2 - 1) as i:
                    for h in range(2):
                        turn(g0 + 2 * i + h + 1, 1 - h)
                        tile_products(g0 + 2 * i + h, 2 * i + h, h)
                turn(g0 + GB - 1, 1)
                for h in range(2):
                    tile_products(g0 + GB - 2 + h, GB - 2 + h, h)

                if b == B - 1:
                    pe.wait_ge(a_done, 1)
                    chosen = route[:, 4, :, :].rearrange("p g e -> p (g e)")
                    nc.tensor.matmul(sc[:, 0, 0, 0:G * E], tri[:, :], chosen, start=True, stop=True)
                    nc.tensor.matmul(sc[:, 1, 0, 0:G * E], ones[:, :], chosen, start=True, stop=True).then_inc(cnt, 1)
                    pe.wait_ge(cnt_read, 1)

                pe.wait_ge(lg_read, g0 + GB)
                pe.wait_ge(copied, 2 * (g0 + GB))
                pe.wait_ge(ab_read, 2 + 24 * b + GB)
                with pe.Fori(0, NB) as i:
                    use = 24 * b + 8 + 8 * i

                    def scores(j):
                        a = g0 + QB * i + j
                        pe.wait_ge(exp_done, a + 1)
                        for c in range(KC):
                            if j == 0:
                                pe.wait_ge(ab_read, use + 2 + c + 1)
                            for m in range(2):
                                last = product(sc[:, j % 2, m, :], t_h[:, c, j * P:(j + 1) * P],
                                               t_l[:, c, j * P:(j + 1) * P],
                                               xt_h[:, c, m * 512:(m + 1) * 512], xt_l[:, c, m * 512:(m + 1) * 512],
                                               c == 0, c == KC - 1)
                        last.then_inc(s_done, 1)

                    def turn_probs(j):
                        a = g0 + QB * i + j
                        pe.wait_ge(exp_done, a + 3)
                        pe.wait_ge(pt_lo, a + 1)
                        transpose_tile(prob[:, 0:KC * P], 0)
                        transpose_tile(prob[:, KC * P:2 * KC * P], 1).then_inc(ptr_done, 1)

                    def attend(j):
                        a = g0 + QB * i + j
                        pe.wait_ge(pt_lo, a + 2)
                        pe.wait_ge(ab_read, use + KC + j + 1)
                        for c in range(GB):
                            last = product(ab[:, j % 2, :], pt_h[:, j % 2, c, :], pt_l[:, j % 2, c, :],
                                           v_h[:, c, :], v_l[:, c, :], c == 0, c == GB - 1)
                        last.then_inc(ab_full, 1)

                    for n in range(KC):
                        pe.wait_ge(ab_read, use + n + 1)
                        for c in range(KC):
                            w = slice(n * P, (n + 1) * P)
                            q = ds(i * (QB * P), QB * P)
                            last = product(ab[:, n % 2, :], mw_h[:, c, w], mw_l[:, c, w], xt_h[:, c, q], xt_l[:, c, q],
                                           c == 0, c == KC - 1)
                        last.then_inc(ab_full, 1)
                    scores(0)
                    scores(1)
                    turn_probs(0)
                    scores(2)
                    turn_probs(1)
                    attend(0)
                    scores(3)
                    turn_probs(2)
                    attend(1)
                    turn_probs(3)
                    attend(2)
                    attend(3)

            def turn_rows(i, h, j, first=False):
                pe.wait_ge(xg_in[h], 16 * j)
                if not first:
                    pe.wait_ge(g_lo, i - 1)
                transpose_tile(xg[:, h, :], h).then_inc(g_t, 1)

            def expert(i, h):
                e = pe.value_load(texp[0:1, ds(i, 1)], min_val=0, max_val=E - 1)
                pe.wait_ge(g_lo, i + 1)
                pe.wait_ge(ab_read, 24 * B + i + 1)
                for c in range(KC):
                    rh = W[:, ds(e, 1), 0, c, :].rearrange("p a n -> p (a n)")
                    rl = W[:, ds(e, 1), 1, c, :].rearrange("p a n -> p (a n)")
                    last = product(ab[:, h, :], st_h[:, h, c, :], st_l[:, h, c, :], rh, rl, c == 0, c == KC - 1)
                last.then_inc(ab_full, 1)

            pe.wait_ge(routed, 1)
            pe.wait_ge(pt_lo, 1 + G)
            turn_rows(0, 0, 1, True)
            for i in range(PEEL):
                turn_rows(i + 1, (i + 1) % 2, (i + 1) // 2 + 1, i == 0)
                pe.wait_ge(w_split, 2 * min(i + 1, EARLY))
                if i >= EARLY:
                    pe.wait_ge(w_lo, i + 1 - EARLY)
                expert(i, i % 2)
            with pe.Fori(PEEL // 2, SLOT_TILES // 2 - 1) as i:
                for h in range(2):
                    turn_rows(2 * i + h + 1, 1 - h, i + 1 + h)
                    expert(2 * i + h, h)
            turn_rows(SLOT_TILES - 1, 1, SLOT_TILES // 2)
            expert(SLOT_TILES - 2, 0)
            expert(SLOT_TILES - 1, 1)

            def turn_comb(g, q, first=False):
                pe.wait_ge(c_done, g + 1)
                if not first:
                    pe.wait_ge(c_lo, g - 1)
                transpose_tile(comb[:, q, :], q % 2).then_inc(c_t, 1)

            def project(g, h):
                pe.wait_ge(c_lo, g + 1)
                pe.wait_ge(ab_read, 24 * B + SLOT_TILES + g + 1)
                for c in range(KC):
                    last = product(ab[:, h, :], st_h[:, h, c, :], st_l[:, h, c, :],
                                   pw_h[:, c, :], pw_l[:, c, :], c == 0, c == KC - 1)
                last.then_inc(ab_full, 1)

            pe.wait_ge(g_lo, SLOT_TILES)
            pe.wait_ge(w_lo, LATE)
            turn_comb(0, 0, True)
            turn_comb(1, 1, True)
            with pe.Fori(0, G // R - 1) as i:
                for q in range(R):
                    project(R * i + q, q % 2)
                    turn_comb(R * i + q + 2, (q + 2) % R)
            for q in range(R):
                project(G - R + q, q % 2)
                if q + 2 < R:
                    turn_comb(G - R + q + 2, q + 2)

    return None


def kernel(**inputs):
    import numpy as np
    import concourse.bacc as bacc
    from concourse.bass_utils import run_bass_kernel_spmd

    a = {k: np.asarray(v) for k, v in inputs.items()}
    x = a["L0_attn_hidden_states"]
    D = x.shape[-1]
    arrays = {
        "x": x,
        "w_qkv": a["L0_attn_w_qkv"],
        "b_qkv": a["L0_attn_b_qkv"].reshape(3, D // P, P).transpose(2, 0, 1),
        "w_out_t": a["L0_attn_w_out"].T,
        "b_out": a["L0_attn_b_out"],
        "router_w": a["L0_ffn_router_w"],
        "router_b": a["L0_ffn_router_b"],
        "expert_w": a["L0_ffn_expert_w"],
        "expert_b": a["L0_ffn_expert_b"],
        "proj_w": a["L0_ffn_proj_w"],
        "proj_b": a["L0_ffn_proj_b"],
        "norm_w": a["L0_ffn_norm_w"],
    }
    arrays = {f"in_{k}": np.ascontiguousarray(v) for k, v in arrays.items()}
    nc = bacc.Bacc("TRN2", target_bir_lowering=False, num_devices=1)
    args = [nc.dram_tensor(k, v.shape, F32, kind="ExternalInput").ap() for k, v in arrays.items()]
    out = nc.dram_tensor("out", x.shape, F32, kind="ExternalOutput").ap()
    gated_attention_moe(nc, *args, out)
    r = run_bass_kernel_spmd(nc, [arrays], core_ids=[0])
    return r.results[0]["out"]
```

```python
from contextlib import ExitStack

import concourse.bass as bass
from concourse import mybir

P = 128
F32 = mybir.dt.float32
F32R = mybir.dt.float32r
I32 = mybir.dt.int32
ALU = mybir.AluOpType
ACT = mybir.ActivationFunctionType
AX = mybir.AxisListType
ds = bass.ds

LN_EPS = 1e-5
RMS_EPS = 1e-6
RSQRT_SEED = float(0x5F3759DF)


class Chain:

    def __init__(self, eng, sem):
        self.eng, self.sem, self.base, self.k, self.total = eng, sem, 0, 0, 0

    def __call__(self, ins):
        self.k += 1
        ins.then_inc(self.sem, 1)
        self.eng.wait_ge(self.sem, self.base + self.k)

    def enter(self, turn, steps):
        self.total = self.base + self.k
        self.base, self.k, self.steps = self.total + turn * steps, 0, steps

    def leave(self, turns):
        assert self.k == self.steps, (self.k, self.steps)
        self.base, self.k = self.total + turns * self.steps, 0


def gated_attention_moe(nc, x, w_qkv, b_qkv, w_out_t, b_out, router_w, router_b,
                        expert_w, expert_b, proj_w, proj_b, norm_w, out):
    B, S, D = x.shape
    E = router_w.shape[1]
    T = B * S
    KC = D // P
    G = T // P
    GB = S // P
    QB = 4
    NB = GB // QB
    NP = E + 2
    SLOT_TILES = 2 * T // P + E
    EARLY = 3
    SCALE = float(D) ** -0.5
    assert D == KC * P == 512 and GB % QB == 0 and SLOT_TILES % 2 == 0

    x_v = x.rearrange("b (t p) h -> b p t h", p=P)
    x_g = x.rearrange("b (t p) h -> (b t) p h", p=P)
    out_g = out.rearrange("b (t p) h -> (b t) p h", p=P)
    wqkv_v = w_qkv.rearrange("(w c p) h -> w p c h", w=3, p=P)
    wout_v = w_out_t.rearrange("(c p) n -> p c n", p=P)
    expert_v = expert_w.rearrange("e (c p) f -> e p c f", p=P)
    proj_v = proj_w.rearrange("(c p) f -> p c f", p=P)

    xn_d = nc.dram_tensor("xn_scratch", (T, D), F32).ap()
    s_d = nc.dram_tensor("s_scratch", (T, D), F32).ap()
    y_d = nc.dram_tensor("y_scratch", (SLOT_TILES * P, D), F32).ap()
    tab_d = nc.dram_tensor("slot_token", (SLOT_TILES * P, 1), I32).ap()
    xn_g = xn_d.rearrange("(g p) h -> g p h", p=P)
    s_g = s_d.rearrange("(g p) h -> g p h", p=P)
    y_g = y_d.rearrange("(g p) h -> g p h", p=P)

    with ExitStack() as ctx:
        def sb(name, shape, dt=F32, stack=ctx):
            return stack.enter_context(nc.sbuf_tensor(name, shape, dt))

        def sem(name):
            return ctx.enter_context(nc.semaphore(name))

        def sems(name, n):
            return [sem(f"{name}{i}") for i in range(n)]

        ident = sb("ident", [P, P])
        ones = sb("ones", [P, P])
        tri = sb("tri", [P, P])
        rank8 = sb("rank8", [P, G, E])
        thr = sb("thr", [P, E, G])
        slot_i = sb("slot_i", [P, SLOT_TILES, E])
        ids = sb("ids", [P, G], I32)
        logits = sb("logits", [P, G, NP])
        bcols = sb("bcols", [P, 3, KC])
        tb = sb("tb", [P, KC])
        stats = sb("stats", [P, GB, 6])
        mean = sb("mean", [P, G])
        rstd = sb("rstd", [P, G])
        shift = sb("shift", [P, G])
        small = sb("small", [P, 12, 16])
        rw = sb("rw", [P, KC, NP])
        rw_h = sb("rw_h", [P, KC, NP], F32R)
        rw_l = sb("rw_l", [P, KC, NP], F32R)
        rb_bc = sb("rb_bc", [P, NP])
        sbias = sb("sbias", [P, D])
        w1 = sb("w1", [P, G])
        w2 = sb("w2", [P, G])
        pos1 = sb("pos1", [P, G], I32)
        pos2 = sb("pos2", [P, G], I32)
        cell1 = sb("cell1", [P, G], I32)
        cell2 = sb("cell2", [P, G], I32)
        token = sb("token", [P, SLOT_TILES], I32)
        texp = sb("texp", [P, SLOT_TILES], I32)
        idx = sb("idx", [P, 8], I32)
        zeros = sb("zeros", [P, SLOT_TILES], I32)
        idv = sb("idv", [P, 1], I32)
        st_h = sb("st_h", [P, 2, KC, P], F32R)
        st_l = sb("st_l", [P, 2, KC, P], F32R)
        xb = sb("xb", [P, GB, D])
        wraw = xb[:, :, :].rearrange("p (a c) n -> p a c n", a=2)
        xn = sb("xn", [P, 2, D])

        with ExitStack() as a:
            wkeep = sb("wkeep", [P, EARLY - 1, 2, KC, D], F32R, a)
            nw_h = sb("nw_h", [P, KC, D], F32R, a)
            nw_l = sb("nw_l", [P, KC, D], F32R, a)
            xt_h = sb("xt_h", [P, KC, S], F32R, a)
            xt_l = sb("xt_l", [P, KC, S], F32R, a)
            v_h = sb("v_h", [P, GB, D], F32R, a)
            v_l = sb("v_l", [P, GB, D], F32R, a)
            mw_h = sb("mw_h", [P, KC, D], F32R, a)
            mw_l = sb("mw_l", [P, KC, D], F32R, a)
            t_h = sb("t_h", [P, KC, QB * P], F32R, a)
            t_l = sb("t_l", [P, KC, QB * P], F32R, a)
            pt_h = sb("pt_h", [P, 2, GB, P], F32R, a)
            pt_l = sb("pt_l", [P, 2, GB, P], F32R, a)
            prob = sb("prob", [P, S], F32, a)
            so = sb("so", [P, 2, D], F32, a)
        with ExitStack() as a:
            raw = [sb(f"raw_{n}", [P, KC, D], F32, a) for n in ("q", "k", "v", "o")]
        with ExitStack() as a:
            sb("raw_qk", [P, 2, KC, D], F32, a)
            xb1 = sb("xb1", [P, GB, D], F32, a)
        xbs = (xb, xb1)
        assert B == 2 and GB == 2 * KC
        with ExitStack() as a:
            W = sb("W", [P, E, 2, KC, D], F32R, a)
            bias_e = sb("bias_e", [P, E, D], F32, a)
            pw_h = sb("pw_h", [P, KC, D], F32R, a)
            pw_l = sb("pw_l", [P, KC, D], F32R, a)
            xg = sb("xg", [P, 2, D], F32, a)
            yt = sb("yt", [P, 2, D], F32, a)
        with ExitStack() as a:
            R, RY = 4, 8
            xf = sb("xf", [P, G, D], F32, a)
            sf = sb("sf", [P, G, D], F32, a)
            y1 = sb("y1", [P, RY, D], F32, a)
            y2 = sb("y2", [P, RY, D], F32, a)
            comb = sb("comb", [P, R, D], F32, a)
            xp = sb("xp", [P, R, D], F32, a)
            yy = sb("yy", [P, R, D], F32, a)
            z = sb("z", [P, R, D], F32, a)
            pb_bc = sb("pb_bc", [P, D], F32, a)
            nrm_bc = sb("nrm_bc", [P, D], F32, a)
            sq = sb("sq", [P, 2, D], F32, a)
        rows = (xn[:, 0, :], xn[:, 1, :], xg[:, 0, :], xg[:, 1, :])
        bvb = prob[:, 0:KC * P].rearrange("p (c n) -> p c n", c=KC)
        bo_bc = so[:, 0, :]
        prod = so[:, 1, 0:KC]
        with ExitStack() as a:
            route = sb("route", [P, 10, G, E], F32, a)
            padded = sb("padded", [P, 2, 2 * G, E], F32, a)
            starts = sb("starts", [P, 2, 2 * E], F32, a)
            slots = sb("slots", [P, SLOT_TILES, E], F32, a)

        sc = ctx.enter_context(nc.psum_tensor("sc", [P, 2, 2, 512], F32))
        tp = ctx.enter_context(nc.psum_tensor("tp", [P, 2, KC, P], F32))
        ab = ctx.enter_context(nc.psum_tensor("ab", [P, 2, D], F32))

        w_in = sems("w_in", 4)
        vec_in = sem("vec_in")
        x_in = sems("x_in", 2)
        const = sem("const")
        zero_out = sem("zero_out")
        fold = sem("fold")
        fold_h = sem("fold_h")
        fold_l = sem("fold_l")
        pre = sem("pre")
        vecs = sem("vecs")
        pre_done = sem("pre_done")
        dv = sem("dv")
        xn_ready = sem("xn_ready")
        xn_st = sems("xn_st", 2)
        t_done = sem("t_done")
        hi_done = sem("hi_done")
        lo_done = sem("lo_done")
        xh_done = sem("xh_done")
        xl_done = sem("xl_done")
        rt_done = sem("rt_done")
        lg_read = sem("lg_read")
        ab_full = sem("ab_full")
        ab_hi = sem("ab_hi")
        ab_read = sem("ab_read")
        s_done = sem("s_done")
        mx = sem("mx")
        exp_done = sem("exp_done")
        ptr_done = sem("ptr_done")
        pt_hi = sem("pt_hi")
        pt_lo = sem("pt_lo")
        so_st = sems("so_st", 2)
        a_done = sem("a_done")
        cnt = sem("cnt")
        gate_d = sem("gate_d")
        gate_e = sem("gate_e")
        routed = sem("routed")
        pl = sem("pl")
        scat = sem("scat")
        we_in = sems("we_in", 2)
        wr_in = sems("wr_in", 2)
        w_split = sem("w_split")
        w_hi = sem("w_hi")
        w_lo = sem("w_lo")
        be_in = sem("be_in")
        ix_in = sem("ix_in")
        xg_in = sems("xg_in", 4)
        g_t = sem("g_t")
        g_hi = sem("g_hi")
        g_lo = sem("g_lo")
        silu_d = sem("silu_d")
        y_st = sems("y_st", 2)
        fin_x = sems("fin_x", G // 4)
        fin_s = sems("fin_s", G // 4)
        vec2_in = sem("vec2_in")
        y_in = sems("y_in", 8)
        c_done = sem("c_done")
        c_t = sem("c_t")
        c_hi = sem("c_hi")
        c_lo = sem("c_lo")
        xp_in = sem("xp_in")
        xp_done = sem("xp_done")
        sq_d = sem("sq_d")
        z_done = sem("z_done")
        g_done = sem("g_done")
        m_done = sem("m_done")
        o_done = sem("o_done")
        o_st = sems("o_st", 4)
        cnt_read = sem("cnt_read")

        block = ctx.enter_context(nc.Block())
        LATE = E - EARLY + 1
        PEEL = E

        @block.sync
        def _(sp):
            sp.sem_inc(so_st[0], 16)
            sp.sem_inc(so_st[1], 16)
            for q in range(R):
                sp.sem_inc(o_st[q], 16)
            for n in (2, 3):
                sp.dma_start(raw[n][:, :, :], wqkv_v[n] if n < 3 else wout_v).then_inc(w_in[n], 16)
            for h in range(2):
                sp.dma_start(xb[:, h * GB // 2:(h + 1) * GB // 2, :], x_v[0][:, h * GB // 2:(h + 1) * GB // 2, :])\
                    .then_inc(x_in[h], 16)
            for n in (0, 1):
                sp.dma_start(raw[n][:, :, :], wqkv_v[n]).then_inc(w_in[n], 16)
            sp.wait_ge(vecs, 1)
            for h in range(2):
                sp.dma_start(xb1[:, h * GB // 2:(h + 1) * GB // 2, :], x_v[1][:, h * GB // 2:(h + 1) * GB // 2, :])\
                    .then_inc(x_in[h], 16)
            for b in range(B):
                with sp.Fori(0, GB // 2) as i:
                    for h in range(2):
                        sp.wait_ge(xn_ready, GB * b + 2 * i + h + 1)
                        sp.dma_start(xn_g[ds(GB * b + 2 * i + h, 1), :, :].rearrange("a p n -> p (a n)"),
                                     xn[:, h, :]).then_inc(xn_st[h], 16)
                with sp.Fori(0, NB) as i:
                    for j in range(QB):
                        sp.wait_ge(ab_read, 2 + 24 * b + 8 + 8 * i + 4 + j + 1)
                        sp.dma_start(s_g[ds(GB * b + QB * i + j, 1), :, :].rearrange("a p n -> p (a n)"),
                                     so[:, j % 2, :]).then_inc(so_st[j % 2], 16)

            def load_late(n):
                e = EARLY + n
                if n < 2:
                    sp.wait_ge(w_split, 2 * (e - 1))
                else:
                    sp.wait_ge(w_lo, n - 1)
                sp.dma_start(wraw[:, e % 2, :, :], expert_v[e] if e < E else proj_v)\
                    .then_inc(wr_in[e % 2], 16)

            def store_y(i, h):
                sp.wait_ge(silu_d, i + 1)
                sp.dma_start(y_g[ds(i, 1), :, :].rearrange("a p n -> p (a n)"), yt[:, h, :])\
                    .then_inc(y_st[h], 16)

            sp.wait_ge(scat, 32 * G)
            sp.dma_start(token[:, :], tab_d.rearrange("(p i) a -> p (i a)", p=P)).then_inc(ix_in, 16)
            sp.wait_ge(s_done, G)
            sp.dma_start(bias_e[:, :, :].rearrange("p e f -> p (e f)"),
                         expert_b.rearrange("e f -> (e f)").rearrange("(a n) -> a n", a=1)
                         .to_broadcast([P, E * D])).then_inc(be_in, 16)
            load_late(0)
            load_late(1)
            for i in range(PEEL):
                if i + 2 < LATE:
                    load_late(i + 2)
                store_y(i, i % 2)
            with sp.Fori(PEEL // 2, SLOT_TILES // 2) as i:
                for h in range(2):
                    store_y(2 * i + h, h)

            sp.wait_ge(ab_full, 24 * B + SLOT_TILES)
            sp.dma_start(pb_bc[:, :], proj_b.rearrange("(a n) -> a n", a=1).to_broadcast([P, D]))\
                .then_inc(vec2_in, 16)
            sp.dma_start(nrm_bc[:, :], norm_w.rearrange("(a n) -> a n", a=1).to_broadcast([P, D]))\
                .then_inc(vec2_in, 16)
            for q in range(2):
                sp.wait_ge(so_st[q], 16 + 8 * G)

            x_all, s_all = (v.rearrange("g p n -> p g n") for v in (x_g, s_g))
            for n in range(G // R):
                w = slice(R * n, R * n + R)
                sp.dma_start(xf[:, w, :], x_all[:, w, :]).then_inc(fin_x[n], 16)
                sp.dma_start(sf[:, w, :], s_all[:, w, :]).then_inc(fin_s[n], 16)
            with sp.Fori(0, G // R) as i:
                for q in range(R):
                    sp.wait_ge(o_done, R * i + q + 1)
                    sp.dma_start(out_g[ds(R * i + q, 1), :, :].rearrange("a p n -> p (a n)"), z[:, q, :])\
                        .then_inc(o_st[q], 16)
            for q in range(R):
                sp.wait_ge(o_st[q], 16 + 16 * (G // R))
            for q in range(2):
                sp.wait_ge(xn_st[q], 8 * G)
                sp.wait_ge(y_st[q], 8 * SLOT_TILES)

        @block.gpsimd
        def _(pool):
            link = Chain(pool, pl)
            pool.memset(ones[:, :], 1.0).then_inc(const, 1)
            link(pool.memset(ident[:, :], 0.0))
            pool.affine_select(out=ident[:, :], in_=ident[:, :], compare_op=ALU.not_equal, fill=1.0,
                               base=0, pattern=[[-1, P]], channel_multiplier=1).then_inc(const, 1)
            pool.wait_ge(const, 1)
            pool.affine_select(out=tri[:, :], in_=ones[:, :], compare_op=ALU.is_gt, fill=0.0,
                               base=0, pattern=[[1, P]], channel_multiplier=-1).then_inc(const, 1)
            pool.iota(rank8[:, :, :], [[0, G], [-1, E]], base=E, channel_multiplier=0,
                      allow_small_or_imprecise_dtypes=True).then_inc(const, 1)
            pool.iota(thr[:, :, :], [[0, E], [P, G]], base=0, channel_multiplier=0,
                      allow_small_or_imprecise_dtypes=True).then_inc(const, 1)
            pool.iota(slot_i[:, :, :], [[1, SLOT_TILES], [0, E]], base=0, channel_multiplier=0,
                      allow_small_or_imprecise_dtypes=True).then_inc(const, 1)
            pool.iota(ids[:, :], [[P, G]], base=0, channel_multiplier=1).then_inc(const, 1)
            link(pool.memset(zeros[:, :], 0))
            pool.dma_start(tab_d.rearrange("(p i) a -> p (i a)", p=P), zeros[:, :]).then_inc(zero_out, 16)
            pool.dma_start(bcols[:, :, :], b_qkv).then_inc(vec_in, 16)
            pool.dma_start(bo_bc, b_out.rearrange("(a n) -> a n", a=1).to_broadcast([P, D])).then_inc(vec_in, 16)
            link(pool.memset(rw[:, :, :], 0.0))
            link(pool.memset(rb_bc[:, :], 0.0))
            pool.dma_start(rw[:, :, 0:E], router_w.rearrange("(c p) e -> p c e", p=P)).then_inc(vec_in, 16)
            pool.dma_start(rb_bc[:, 0:E], router_b.rearrange("(a n) -> a n", a=1).to_broadcast([P, E]))\
                .then_inc(vec_in, 16)
            pool.wait_ge(routed, 1)
            pool.wait_ge(zero_out, 16)
            for g in range(G):
                for pos in (cell1, cell2):
                    pool.indirect_dma_start(tab_d, bass.IndirectOffsetOnAxis(pos[:, g:g + 1], 0),
                                            ids[:, g:g + 1], None).then_inc(scat, 16)
            for e in range(2):
                pool.dma_start(wraw[:, e, :, :], expert_v[e]).then_inc(we_in[e % 2], 16)
            for e in range(EARLY):
                pool.wait_ge(we_in[e % 2], 16 * (e // 2 + 1))
                pool.tensor_copy(W[:, e, 0, :, :], wraw[:, e % 2, :, :]).then_inc(w_split, 1)
                pool.wait_ge(w_split, 2 * e + 1)
                pool.tensor_tensor(W[:, e, 1, :, :], wraw[:, e % 2, :, :], W[:, e, 0, :, :], ALU.subtract)\
                    .then_inc(w_split, 1)
                if e + 2 < EARLY:
                    pool.wait_ge(w_split, 2 * e + 2)
                    pool.dma_start(wraw[:, e % 2, :, :], expert_v[e + 2]).then_inc(we_in[e % 2], 16)

            def gather(i, q):
                link(pool.tensor_copy(idx[:, q:q + 1], token[:, ds(i, 1)]))
                pool.nop(nofuse=True)
                pool.indirect_dma_start(rows[q], None, xn_d,
                                        bass.IndirectOffsetOnAxis(idx[:, q:q + 1], 0)).then_inc(xg_in[q], 16)

            for q in range(2):
                pool.wait_ge(xn_st[q], 8 * G)
            pool.wait_ge(ix_in, 16)
            gather(0, 0)
            gather(1, 1)
            pool.wait_ge(ptr_done, 1 + G)
            gather(2, 2)
            gather(3, 3)
            with pool.Fori(0, SLOT_TILES // 4 - 1) as i:
                link.enter(i, 4)
                for q in range(4):
                    pool.wait_ge(g_t, 4 * i + q + 1)
                    gather(4 * i + q + 4, q)
            link.leave(SLOT_TILES // 4 - 1)
            for q in range(2):
                pool.wait_ge(y_st[q], 8 * SLOT_TILES)

            def gather_y(g, q):
                for n, y in enumerate((y1, y2)):
                    pool.indirect_dma_start(y[:, q, :], None, y_d,
                                            bass.IndirectOffsetOnAxis((pos1, pos2)[n][:, g:g + 1], 0))\
                        .then_inc(y_in[q], 16)

            def residual(g, q):
                pool.wait_ge(xp_in, g + 1)
                pool.tensor_tensor(xp[:, q, :], xp[:, q, :], pb_bc[:, :], ALU.add).then_inc(xp_done, 1)

            def add_x(g, q):
                pool.wait_ge(m_done, g + 1)
                pool.tensor_tensor(z[:, q, :], z[:, q, :], xf[:, ds(g, 1), :].rearrange("p a n -> p (a n)"), ALU.add)\
                    .then_inc(o_done, 1)

            for q in range(RY):
                gather_y(q, q)
            pool.wait_ge(vec2_in, 32)
            residual(0, 0)
            for g in range(G):
                if g + 1 < G:
                    residual(g + 1, (g + 1) % R)
                if g + RY < G:
                    pool.wait_ge(c_done, g + 1)
                    gather_y(g + RY, g % RY)
                if g >= 2:
                    add_x(g - 2, (g - 2) % R)
            for q in range(2):
                add_x(G - 2 + q, R - 2 + q)

        @block.scalar
        def _(act):
            act.sem_inc(exp_done, 2)

            def fold_high(n):
                act.wait_ge(fold, n + 1)
                dst = (nw_h if n < KC else mw_h)[:, n % KC, :]
                nc.scalar.copy(dst, sc[:, (n % 4) // 2, n % 2, :]).then_inc(fold_h, 1)

            for n in range(KC):
                fold_high(n)

            for b in range(B):
                def hi(g, t, h):
                    act.wait_ge(t_done, g + 1)
                    nc.scalar.copy(st_h[:, h, :, :], tp[:, h, :, :]).then_inc(hi_done, 1)
                    act.wait_ge(hi_done, g + 1)
                    nc.scalar.copy(xt_h[:, :, ds(t * P, P)], st_h[:, h, :, :]).then_inc(xh_done, 1)

                def v_hi(g, t, h):
                    act.wait_ge(ab_full, 24 * b + t + 1)
                    nc.scalar.copy(v_h[:, ds(t, 1), :].rearrange("p a n -> p (a n)"), ab[:, h, :]).then_inc(ab_hi, 1)

                g0 = GB * b
                hi(g0, 0, 0)
                hi(g0 + 1, 1, 1)
                with act.Fori(0, GB // 2 - 1) as i:
                    for h in range(2):
                        v_hi(g0 + 2 * i + h, 2 * i + h, h)
                        hi(g0 + 2 * i + h + 2, 2 * i + h + 2, h)
                for h in range(2):
                    v_hi(g0 + GB - 2 + h, GB - 2 + h, h)

                if b == 0:
                    for n in range(KC, 2 * KC):
                        fold_high(n)
                if b == B - 1:
                    act.wait_ge(gate_d, 1)
                    nc.scalar.activation(small[:, 10, :], small[:, 9, :], ACT.Exp).then_inc(gate_e, 1)

                with act.Fori(0, NB) as i:
                    for c in range(KC):
                        act.wait_ge(ab_full, 24 * b + 8 + 8 * i + c + 1)
                        nc.scalar.activation(t_h[:, c, :], ab[:, c % 2, :], ACT.Identity, bias=tb[:, c:c + 1])\
                            .then_inc(ab_hi, 1)

                    def pt_split(j):
                        act.wait_ge(ptr_done, 1 + g0 + QB * i + j + 1)
                        nc.scalar.copy(pt_h[:, j % 2, :, :], tp[:, :, :, :].rearrange("p a c n -> p (a c) n"))\
                            .then_inc(pt_hi, 1)

                    for j in range(QB):
                        if j >= 1:
                            pt_split(j - 1)
                        act.wait_ge(mx, g0 + QB * i + j + 1)
                        act.wait_ge(ptr_done, g0 + QB * i + j + 1)
                        nc.scalar.activation(prob[:, :], sc[:, j % 2, :, :].rearrange("p a n -> p (a n)"), ACT.Exp,
                                             bias=small[:, 4 + j, 1:2], scale=SCALE,
                                             accum_out=small[:, 4 + j, 2:3]).then_inc(exp_done, 1)
                    pt_split(QB - 1)

            def g_split(i, h):
                act.wait_ge(g_t, i + 1)
                nc.scalar.copy(st_h[:, h, :, :], tp[:, h, :, :]).then_inc(g_hi, 1)

            def silu(i, h):
                act.wait_ge(ab_read, 2 + 24 * B + i + 1)
                nc.scalar.activation(yt[:, h, :], yt[:, h, :], ACT.Silu).then_inc(silu_d, 1)

            def w_high(n):
                e = EARLY + n
                act.wait_ge(wr_in[e % 2], 16 * (n // 2 + 1))
                dst = W[:, e, 0, :, :] if e < E else pw_h[:, :, :]
                nc.scalar.copy(dst, wraw[:, e % 2, :, :]).then_inc(w_hi, 1)

            act.wait_ge(ab_full, 24 * B)
            act.wait_ge(xl_done, G)
            g_split(0, 0)
            for i in range(PEEL):
                if i < LATE:
                    w_high(i)
                g_split(i + 1, (i + 1) % 2)
                silu(i, i % 2)
            with act.Fori(PEEL // 2, SLOT_TILES // 2 - 1) as i:
                for h in range(2):
                    g_split(2 * i + h + 1, 1 - h)
                    silu(2 * i + h, h)
            g_split(SLOT_TILES - 1, 1)
            silu(SLOT_TILES - 2, 0)
            silu(SLOT_TILES - 1, 1)

            def c_split(g, h):
                act.wait_ge(c_t, g + 1)
                nc.scalar.copy(st_h[:, h, :, :], tp[:, h, :, :]).then_inc(c_hi, 1)

            def squares(g, q):
                act.wait_ge(ab_read, 2 + 24 * B + SLOT_TILES + g + 1)
                nc.scalar.activation(sq[:, q % 2, :], yy[:, q, :], ACT.Square,
                                     accum_out=small[:, 0, q:q + 1]).then_inc(sq_d, 1)

            def gate(g, q):
                act.wait_ge(z_done, g + 1)
                nc.scalar.activation(z[:, q, :], z[:, q, :], ACT.Silu).then_inc(g_done, 1)

            def normalise(g, q):
                nc.scalar.activation(xp[:, q, :], xf[:, ds(g, 1), :].rearrange("p a n -> p (a n)"), ACT.Identity, bias=shift[:, ds(g, 1)],
                                     scale=rstd[:, ds(g, 1)]).then_inc(xp_in, 1)

            def last_pair(g, q, more=True):
                for k in range(2):
                    if more:
                        normalise(g + k + 2, (q + k + 2) % R)
                    squares(g + k, q + k)
                    if more:
                        c_split(g + k + 2, k)
                gate(g, q)
                gate(g + 1, q + 1)

            for n in range(G // R):
                act.wait_ge(fin_x[n], 16)
            normalise(0, 0)
            normalise(1, 1)
            c_split(0, 0)
            c_split(1, 1)
            with act.Fori(0, G // R - 1) as i:
                last_pair(R * i, 0)
                last_pair(R * i + 2, 2)
            last_pair(G - R, 0)
            last_pair(G - 2, 2, more=False)

        @block.vector
        def _(dve):
            link = Chain(dve, dv)
            vec = nc.vector

            def rsqrt(r, v, t):
                link(vec.tensor_scalar(r.bitcast(I32), v.bitcast(I32), 1, None, ALU.logical_shift_right))
                link(vec.tensor_scalar(r.bitcast(I32), r.bitcast(I32), -1.0, RSQRT_SEED, ALU.mult, ALU.add))
                for _ in range(3):
                    link(vec.tensor_tensor(t, r, r, ALU.mult))
                    link(vec.tensor_tensor(t, t, v, ALU.mult))
                    link(vec.tensor_scalar(t, t, -0.5, 1.5, ALU.mult, ALU.add))
                    link(vec.tensor_tensor(r, r, t, ALU.mult))

            dve.sem_inc(ab_read, 2)
            dve.sem_inc(pt_lo, 1)
            dve.wait_ge(vec_in, 64)
            dve.wait_ge(const, 7)
            vec.tensor_tensor(prod, bcols[:, 0, :], bcols[:, 1, :], ALU.mult).then_inc(pre, 1)
            for c in range(KC):
                vec.tensor_scalar(bvb[:, c, :], ones[:, :], bcols[:, 2, c:c + 1], None, ALU.mult).then_inc(pre, 1)

            def batch_stats(b):
                g0 = GB * b
                for h in range(2):
                    dve.wait_ge(x_in[h], 16 * (b + 1))
                    with dve.Fori(0, GB // 2) as t:
                        link.enter(t, 1)
                        link(vec.bn_stats(stats[:, ds(t + h * (GB // 2), 1), :].rearrange("p a s -> p (a s)"),
                                          xbs[b][:, ds(t + h * (GB // 2), 1), :].rearrange("p a n -> p (a n)")))
                    link.leave(GB // 2)
                me, mo = stats[:, :, 1], stats[:, :, 4]
                ve, vo = stats[:, :, 2], stats[:, :, 5]
                m, r = mean[:, g0:g0 + GB], rstd[:, g0:g0 + GB]
                a, v = small[:, 0, 0:GB], small[:, 1, 0:GB]
                link(vec.tensor_tensor(a, me, mo, ALU.subtract))
                link(vec.tensor_tensor(a, a, a, ALU.mult))
                link(vec.tensor_tensor(v, ve, vo, ALU.add))
                link(vec.tensor_scalar(a, a, 0.25, LN_EPS, ALU.mult, ALU.add))
                link(vec.scalar_tensor_tensor(v, v, 1.0 / D, a, ALU.mult, ALU.add))
                link(vec.tensor_tensor(m, me, mo, ALU.add))
                link(vec.tensor_scalar(m, m, 0.5, None, ALU.mult))
                rsqrt(r, v, a)
                link(vec.scalar_tensor_tensor(shift[:, g0:g0 + GB], m, -1.0, r, ALU.mult, ALU.mult))

            def normalise(b, t, h, first=False):
                g = GB * b + t
                if not first:
                    dve.wait_ge(t_done, g - 1)
                    dve.wait_ge(xn_st[h], 8 * (g - h))
                vec.tensor_scalar(xn[:, h, :], xbs[b][:, ds(t, 1), :].rearrange("p a n -> p (a n)"),
                                  mean[:, ds(g, 1)], rstd[:, ds(g, 1)], ALU.subtract, ALU.mult).then_inc(xn_ready, 1)

            def lo(b, t, h):
                g = GB * b + t
                dve.wait_ge(hi_done, g + 1)
                vec.tensor_tensor(st_l[:, h, :, :], tp[:, h, :, :], st_h[:, h, :, :], ALU.subtract).then_inc(lo_done, 1)
                dve.wait_ge(lo_done, g + 1)
                vec.tensor_copy(xt_l[:, :, ds(t * P, P)], st_l[:, h, :, :]).then_inc(xl_done, 1)

            def read_logits(g, h):
                dve.wait_ge(rt_done, g + 1)
                vec.tensor_tensor(logits[:, ds(g, 1), :].rearrange("p a n -> p (a n)"), sc[:, h, 0, 0:NP],
                                  rb_bc[:, :], ALU.add).then_inc(lg_read, 1)

            def v_lo(b, t, h):
                dve.wait_ge(ab_hi, 16 * b + t + 1)
                vec.tensor_tensor(v_l[:, ds(t, 1), :].rearrange("p a n -> p (a n)"), ab[:, h, :],
                                  v_h[:, ds(t, 1), :].rearrange("p a n -> p (a n)"), ALU.subtract).then_inc(ab_read, 1)

            def fold_low(n):
                dve.wait_ge(fold_h, n + 1)
                h, l = (nw_h, nw_l) if n < KC else (mw_h, mw_l)
                vec.tensor_tensor(l[:, n % KC, :], sc[:, (n % 4) // 2, n % 2, :], h[:, n % KC, :], ALU.subtract)\
                    .then_inc(fold_l, 1)

            def fold_biases():
                dve.wait_ge(vecs, 1)
                vec.tensor_copy(tb[:, :], ab[:, 0, 0:KC]).then_inc(pre_done, 1)
                link(vec.tensor_copy(rw[:, :, E], ab[:, 0, KC:2 * KC]))
                vec.tensor_reduce(rb_bc[:, E:E + 1], ab[:, 0, 2 * KC:3 * KC], AX.X, ALU.add).then_inc(pre_done, 1)
                link(vec.tensor_tensor(sbias[:, :], ab[:, 1, :], bo_bc, ALU.add))
                link(vec.tensor_copy(rw_h[:, :, :], rw[:, :, :]))
                vec.tensor_tensor(rw_l[:, :, :], rw[:, :, :], rw_h[:, :, :], ALU.subtract).then_inc(pre_done, 1)
                dve.wait_ge(pre_done, 3)

            def choose():
                dve.wait_ge(lg_read, G)
                L = logits[:, :, 0:E]
                row = lambda n: small[:, n, :]
                wide = lambda n: route[:, n, :, :]
                per_token = lambda v: v.unsqueeze(2).to_broadcast([P, G, E])

                def best(values, top, last, onehot):
                    link(vec.tensor_reduce(top, values, AX.X, ALU.max))
                    link(vec.tensor_tensor(wide(0), values, per_token(top), ALU.is_equal))
                    link(vec.tensor_tensor(wide(0), wide(0), rank8[:, :, :], ALU.mult))
                    link(vec.tensor_reduce(last, wide(0), AX.X, ALU.max))
                    link(vec.tensor_tensor(onehot, rank8[:, :, :], per_token(last), ALU.is_equal))

                best(L, row(0), row(1), wide(1))
                link(vec.scalar_tensor_tensor(wide(2), wide(1), -3e38, L, ALU.mult, ALU.add))
                best(wide(2), row(2), row(1), wide(3))
                vec.tensor_tensor(wide(4), wide(1), wide(3), ALU.add).then_inc(a_done, 1)
                vec.tensor_tensor(row(9), row(2), row(0), ALU.subtract).then_inc(gate_d, 1)
                link(vec.memset(padded[:, :, :, :], 0.0))
                link(vec.memset(starts[:, :, :], 0.0))
                dve.wait_ge(cnt, 1)
                link(vec.tensor_copy(wide(5), sc[:, 0, 0, 0:G * E].rearrange("p (g e) -> p g e", e=E)))
                link(vec.tensor_copy(wide(6), sc[:, 1, 0, 0:G * E].rearrange("p (g e) -> p g e", e=E)))
                vec.tensor_copy(padded[:, 0, G:2 * G, :], wide(6)).then_inc(cnt_read, 1)
                dve.wait_ge(cnt_read, 1)
                dve.wait_ge(gate_e, 1)
                link(vec.tensor_scalar(row(11), row(10), 1.0, None, ALU.add))
                link(vec.reciprocal(w1[:, :], row(11)))
                link(vec.tensor_tensor(w2[:, :], w1[:, :], row(10), ALU.mult))
                src, back = 0, 1
                while back < G:
                    link(vec.tensor_tensor(padded[:, 1 - src, G:2 * G, :], padded[:, src, G:2 * G, :],
                                           padded[:, src, G - back:2 * G - back, :], ALU.add))
                    src, back = 1 - src, 2 * back
                link(vec.tensor_tensor(wide(7), padded[:, src, G:2 * G, :], wide(6), ALU.subtract))
                total = padded[:, src, 2 * G - 1, :]
                by_tile = wide(8).rearrange("p g e -> p (g e)").rearrange("p (e g) -> p e g", e=E)
                link(vec.scalar_tensor_tensor(by_tile, total.unsqueeze(2).to_broadcast([P, E, G]), 1.0, thr[:, :, :],
                                              ALU.max, ALU.is_gt))
                n_tiles, first = small[:, 8, 0:E], small[:, 11, 0:E]
                link(vec.tensor_reduce(n_tiles, by_tile, AX.X, ALU.add))
                link(vec.tensor_copy(starts[:, 0, E:2 * E], n_tiles))
                src, back = 0, 1
                while back < E:
                    link(vec.tensor_tensor(starts[:, 1 - src, E:2 * E], starts[:, src, E:2 * E],
                                           starts[:, src, E - back:2 * E - back], ALU.add))
                    src, back = 1 - src, 2 * back
                link(vec.tensor_tensor(first, starts[:, src, E:2 * E], n_tiles, ALU.subtract))
                link(vec.tensor_tensor(slots[:, :, :], slot_i[:, :, :],
                                       first.unsqueeze(1).to_broadcast([P, SLOT_TILES, E]), ALU.is_ge))
                of_tile = wide(9).rearrange("p g e -> p (g e)")[:, 0:SLOT_TILES]
                link(vec.tensor_reduce(of_tile, slots[:, :, :], AX.X, ALU.add))
                link(vec.tensor_scalar(texp[:, :], of_tile, -1.0, None, ALU.add))
                link(vec.scalar_tensor_tensor(wide(7), first.unsqueeze(1).to_broadcast([P, G, E]), float(P), wide(7),
                                              ALU.mult, ALU.add))
                link(vec.tensor_tensor(wide(7), wide(7), wide(5), ALU.add))
                for onehot, pos in ((wide(1), pos1), (wide(3), pos2)):
                    link(vec.tensor_tensor(wide(8), wide(7), onehot, ALU.mult))
                    link(vec.tensor_reduce(row(1), wide(8), AX.X, ALU.add))
                    link(vec.tensor_copy(pos[:, :], row(1)))
                    at, cell = row(2).bitcast(I32), (cell1 if pos is pos1 else cell2)
                    link(vec.tensor_scalar(at, pos[:, :], P - 1, None, ALU.bitwise_and))
                    link(vec.tensor_scalar(cell[:, :], pos[:, :], P.bit_length() - 1, None, ALU.logical_shift_right))
                    link(vec.scalar_tensor_tensor(cell[:, :], at, float(SLOT_TILES), cell[:, :], ALU.mult, ALU.add))
                dve.sem_inc(routed, 1)

            batch_stats(0)
            normalise(0, 0, 0, True)
            normalise(0, 1, 1, True)
            for n in range(KC):
                fold_low(n)
            fold_biases()
            for b in range(B):
                g0 = GB * b
                lo(b, 0, 0)
                with dve.Fori(0, GB // 2 - 1) as i:
                    for h in range(2):
                        t = 2 * i + h
                        normalise(b, t + 2, h)
                        lo(b, t + 1, 1 - h)
                        read_logits(g0 + t, h)
                        v_lo(b, t, h)
                lo(b, GB - 1, 1)
                for h in range(2):
                    read_logits(g0 + GB - 2 + h, h)
                    v_lo(b, GB - 2 + h, h)

                if b + 1 < B:
                    batch_stats(b + 1)
                    normalise(b + 1, 0, 0)
                    normalise(b + 1, 1, 1)
                    for n in range(KC, 2 * KC):
                        fold_low(n)
                if b == B - 1:
                    choose()

                dve.wait_ge(lg_read, g0 + GB)
                with dve.Fori(0, NB) as i:
                    link.enter(i, 3 * QB)
                    for c in range(KC):
                        dve.wait_ge(ab_hi, 16 * b + 8 + KC * i + c + 1)
                        vec.scalar_tensor_tensor(t_l[:, c, :], ab[:, c % 2, :], tb[:, c:c + 1], t_h[:, c, :],
                                                 ALU.add, ALU.subtract).then_inc(ab_read, 1)

                    def row_max(j):
                        n = g0 + QB * i + j
                        key = logits[:, ds(n, 1), E:E + 1].rearrange("p a n -> p (a n)")
                        dve.wait_ge(s_done, n + 1)
                        link(vec.tensor_reduce(small[:, 4 + j, 0:1], sc[:, j % 2, :, :], AX.XY, ALU.max, negate=True))
                        link(vec.tensor_tensor(small[:, 4 + j, 1:2], small[:, 4 + j, 0:1], key, ALU.subtract))
                        vec.tensor_scalar(small[:, 4 + j, 1:2], small[:, 4 + j, 1:2], key, SCALE, ALU.add, ALU.mult)\
                            .then_inc(mx, 1)

                    def pt_low(j):
                        dve.wait_ge(pt_hi, g0 + QB * i + j + 1)
                        vec.tensor_tensor(pt_l[:, j % 2, :, :], tp[:, :, :, :].rearrange("p a c n -> p (a c) n"),
                                          pt_h[:, j % 2, :, :], ALU.subtract).then_inc(pt_lo, 1)

                    def attn_out(j):
                        dve.wait_ge(ab_full, 24 * b + 8 + 8 * i + 4 + j + 1)
                        link(vec.reciprocal(small[:, 4 + j, 3:4], small[:, 4 + j, 2:3]))
                        dve.wait_ge(so_st[j % 2], 8 * g0 + 32 * i + 16 * (j // 2) + 16)
                        vec.scalar_tensor_tensor(so[:, j % 2, :], ab[:, j % 2, :], small[:, 4 + j, 3:4], sbias[:, :],
                                                 ALU.mult, ALU.add).then_inc(ab_read, 1)

                    row_max(0)
                    row_max(1)
                    pt_low(0)
                    row_max(2)
                    pt_low(1)
                    attn_out(0)
                    row_max(3)
                    pt_low(2)
                    attn_out(1)
                    pt_low(3)
                    attn_out(2)
                    attn_out(3)
                link.leave(NB)

            def w_low(n):
                e = EARLY + n
                dve.wait_ge(w_hi, n + 1)
                hi_part, dst = (W[:, e, 0, :, :], W[:, e, 1, :, :]) if e < E else (pw_h[:, :, :], pw_l[:, :, :])
                vec.tensor_tensor(dst, wraw[:, e % 2, :, :], hi_part, ALU.subtract).then_inc(w_lo, 1)

            def g_low(i, h):
                dve.wait_ge(g_hi, i + 1)
                vec.tensor_tensor(st_l[:, h, :, :], tp[:, h, :, :], st_h[:, h, :, :], ALU.subtract).then_inc(g_lo, 1)

            def add_bias(i, h, first=False):
                e = dve.value_load(texp[0:1, ds(i, 1)], min_val=0, max_val=E - 1)
                dve.wait_ge(ab_full, 24 * B + i + 1)
                if not first:
                    dve.wait_ge(y_st[h], 8 * (i - h))
                vec.tensor_tensor(yt[:, h, :], ab[:, h, :], bias_e[:, ds(e, 1), :].rearrange("p a n -> p (a n)"),
                                  ALU.add).then_inc(ab_read, 1)

            for q in range(2):
                dve.wait_ge(so_st[q], 16 + 8 * G)
            dve.wait_ge(be_in, 16)
            g_low(0, 0)
            for i in range(PEEL):
                if i < LATE:
                    w_low(i)
                g_low(i + 1, (i + 1) % 2)
                add_bias(i, i % 2, i < 2)
            with dve.Fori(PEEL // 2, SLOT_TILES // 2 - 1) as i:
                for h in range(2):
                    g_low(2 * i + h + 1, 1 - h)
                    add_bias(2 * i + h, h)
            g_low(SLOT_TILES - 1, 1)
            add_bias(SLOT_TILES - 2, 0)
            add_bias(SLOT_TILES - 1, 1)

            def combine(g, q):
                dve.wait_ge(y_in[q], 4 * (g - q) + 32)
                link(vec.tensor_scalar(y1[:, q, :], y1[:, q, :], w1[:, ds(g, 1)], None, ALU.mult))
                vec.scalar_tensor_tensor(comb[:, q % R, :], y2[:, q, :], w2[:, ds(g, 1)], y1[:, q, :],
                                         ALU.mult, ALU.add).then_inc(c_done, 1)

            def c_low(g, h):
                dve.wait_ge(c_hi, g + 1)
                vec.tensor_tensor(st_l[:, h, :, :], tp[:, h, :, :], st_h[:, h, :, :], ALU.subtract).then_inc(c_lo, 1)

            def add_product(g, q):
                dve.wait_ge(xp_done, g + 1)
                dve.wait_ge(ab_full, 24 * B + SLOT_TILES + g + 1)
                vec.tensor_tensor(yy[:, q, :], ab[:, q % 2, :], xp[:, q, :], ALU.add).then_inc(ab_read, 1)

            def last_pair(g, q, more=True):
                for k in range(2):
                    if more:
                        combine(g + k + 2, (q + k + 2) % RY)
                    add_product(g + k, (q + k) % R)
                    if more:
                        c_low(g + k + 2, k)
                q = q % R
                ms, r, t = (small[:, n, q:q + 2] for n in (1, 2, 3))
                dve.wait_ge(sq_d, g + 2)
                link(vec.tensor_scalar(ms, small[:, 0, q:q + 2], 1.0 / D, RMS_EPS, ALU.mult, ALU.add))
                rsqrt(r, ms, t)
                for k in range(2):
                    dve.wait_ge(o_st[q + k], 4 * (g - q) + 16)
                    vec.scalar_tensor_tensor(z[:, q + k, :], yy[:, q + k, :], r[:, k:k + 1], nrm_bc[:, :],
                                             ALU.mult, ALU.mult).then_inc(z_done, 1)
                for k in range(2):
                    dve.wait_ge(g_done, g + k + 1)
                    vec.tensor_tensor(z[:, q + k, :], z[:, q + k, :],
                                      sf[:, ds(g + k, 1), :].rearrange("p a n -> p (a n)"), ALU.mult).then_inc(m_done, 1)

            dve.wait_ge(vec2_in, 32)
            for n in range(G // R):
                dve.wait_ge(fin_s[n], 16)
            combine(0, 0)
            combine(1, 1)
            c_low(0, 0)
            c_low(1, 1)
            for g in range(0, G, 2):
                last_pair(g, g % RY, more=g + 2 < G)

        @block.tensor
        def _(pe):
            def product(dst, lh, ll, rh, rl, start, stop):
                nc.tensor.matmul(dst, lh, rh, start=start, stop=False)
                nc.tensor.matmul(dst, lh, rl, start=False, stop=False)
                return nc.tensor.matmul(dst, ll, rh, start=False, stop=stop)

            def transpose_tile(src, h):
                for c in range(KC):
                    last = nc.tensor.transpose(tp[:, h, c, :], src[:, c * P:(c + 1) * P], ident[:, :])
                return last

            pe.sem_inc(ptr_done, 1)
            def fold_weights(first, left, right):
                for n in range(first, first + KC):
                    for c in range(KC):
                        last = nc.tensor.matmul(sc[:, (n % 4) // 2, n % 2, :], left[:, c, (n % KC) * P:(n % KC + 1) * P],
                                                right[:, c, :], start=(c == 0), stop=(c == KC - 1))
                    last.then_inc(fold, 1)

            for n in (2, 3):
                pe.wait_ge(w_in[n], 16)
            fold_weights(0, raw[2], raw[3])
            pe.wait_ge(pre, 1 + KC)
            for n in (0, 1):
                pe.wait_ge(w_in[n], 16)
            for m, (left, col) in enumerate(((raw[1], 0), (raw[0], 1))):
                for n in range(KC):
                    for c in range(KC):
                        nc.tensor.matmul(ab[:, 0, m * KC + n:m * KC + n + 1], left[:, c, n * P:(n + 1) * P],
                                         bcols[:, col, c:c + 1], start=(c == 0), stop=(c == KC - 1))
            nc.tensor.matmul(ab[:, 0, 2 * KC:3 * KC], ones[:, :], prod, start=True, stop=True)
            for c in range(KC):
                last = nc.tensor.matmul(ab[:, 1, :], bvb[:, c, :], raw[3][:, c, :], start=(c == 0), stop=(c == KC - 1))
            last.then_inc(vecs, 1)

            for b in range(B):
                g0 = GB * b

                def turn(g, h, first=False):
                    pe.wait_ge(xn_ready, g + 1)
                    if not first:
                        pe.wait_ge(lo_done, g - 1)
                    transpose_tile(xn[:, h, :], h).then_inc(t_done, 1)

                def tile_products(g, t, h, first=False):
                    pe.wait_ge(lo_done, g + 1)
                    if not first:
                        pe.wait_ge(lg_read, g - 1)
                    for c in range(KC):
                        last = product(sc[:, h, 0, 0:NP], st_h[:, h, c, :], st_l[:, h, c, :],
                                       rw_h[:, c, :], rw_l[:, c, :], c == 0, c == KC - 1)
                    last.then_inc(rt_done, 1)
                    pe.wait_ge(ab_read, 24 * b + t + 1)
                    for c in range(KC):
                        last = product(ab[:, h, :], st_h[:, h, c, :], st_l[:, h, c, :],
                                       nw_h[:, c, :], nw_l[:, c, :], c == 0, c == KC - 1)
                    last.then_inc(ab_full, 1)

                if b:
                    pe.wait_ge(pt_lo, 1 + g0)
                turn(g0, 0, b == 0)
                if b == 0:
                    pe.wait_ge(fold_l, KC)
                    pe.wait_ge(pre_done, 3)
                else:
                    pe.wait_ge(exp_done, 2 + g0)
                for h in range(2):
                    turn(g0 + h + 1, 1 - h, b == 0 and h == 0)
                    tile_products(g0 + h, h, h, b == 0)
                with pe.Fori(1, GB // 2 - 1) as i:
                    for h in range(2):
                        turn(g0 + 2 * i + h + 1, 1 - h)
                        tile_products(g0 + 2 * i + h, 2 * i + h, h)
                turn(g0 + GB - 1, 1)
                for h in range(2):
                    tile_products(g0 + GB - 2 + h, GB - 2 + h, h)

                if b == 0:
                    pe.wait_ge(lg_read, GB)
                    fold_weights(KC, raw[0], raw[1])
                    pe.wait_ge(fold_l, 2 * KC)
                if b == B - 1:
                    pe.wait_ge(a_done, 1)
                    chosen = route[:, 4, :, :].rearrange("p g e -> p (g e)")
                    nc.tensor.matmul(sc[:, 0, 0, 0:G * E], tri[:, :], chosen, start=True, stop=True)
                    nc.tensor.matmul(sc[:, 1, 0, 0:G * E], ones[:, :], chosen, start=True, stop=True).then_inc(cnt, 1)
                    pe.wait_ge(cnt_read, 1)

                pe.wait_ge(lg_read, g0 + GB)
                pe.wait_ge(xh_done, g0 + GB)
                pe.wait_ge(xl_done, g0 + GB)
                pe.wait_ge(ab_read, 2 + 24 * b + GB)
                with pe.Fori(0, NB) as i:
                    use = 24 * b + 8 + 8 * i

                    def scores(j):
                        a = g0 + QB * i + j
                        pe.wait_ge(exp_done, a + 1)
                        for c in range(KC):
                            if j == 0:
                                pe.wait_ge(ab_read, use + 2 + c + 1)
                            for m in range(2):
                                last = product(sc[:, j % 2, m, :], t_h[:, c, j * P:(j + 1) * P],
                                               t_l[:, c, j * P:(j + 1) * P],
                                               xt_h[:, c, m * 512:(m + 1) * 512], xt_l[:, c, m * 512:(m + 1) * 512],
                                               c == 0, c == KC - 1)
                        last.then_inc(s_done, 1)

                    def turn_probs(j):
                        a = g0 + QB * i + j
                        pe.wait_ge(exp_done, a + 3)
                        pe.wait_ge(pt_lo, a + 1)
                        transpose_tile(prob[:, 0:KC * P], 0)
                        transpose_tile(prob[:, KC * P:2 * KC * P], 1).then_inc(ptr_done, 1)

                    def attend(j):
                        a = g0 + QB * i + j
                        pe.wait_ge(pt_lo, a + 2)
                        pe.wait_ge(ab_read, use + KC + j + 1)
                        for c in range(GB):
                            last = product(ab[:, j % 2, :], pt_h[:, j % 2, c, :], pt_l[:, j % 2, c, :],
                                           v_h[:, c, :], v_l[:, c, :], c == 0, c == GB - 1)
                        last.then_inc(ab_full, 1)

                    for n in range(KC):
                        pe.wait_ge(ab_read, use + n + 1)
                        for c in range(KC):
                            w = slice(n * P, (n + 1) * P)
                            q = ds(i * (QB * P), QB * P)
                            last = product(ab[:, n % 2, :], mw_h[:, c, w], mw_l[:, c, w], xt_h[:, c, q], xt_l[:, c, q],
                                           c == 0, c == KC - 1)
                        last.then_inc(ab_full, 1)
                    scores(0)
                    scores(1)
                    turn_probs(0)
                    scores(2)
                    turn_probs(1)
                    attend(0)
                    scores(3)
                    turn_probs(2)
                    attend(1)
                    turn_probs(3)
                    attend(2)
                    attend(3)

            def turn_rows(i, q, j, first=False):
                pe.wait_ge(xg_in[q], 16 * (j + 1))
                if not first:
                    pe.wait_ge(g_lo, i - 1)
                transpose_tile(rows[q], q % 2).then_inc(g_t, 1)

            def expert(i, h):
                e = pe.value_load(texp[0:1, ds(i, 1)], min_val=0, max_val=E - 1)
                pe.wait_ge(g_lo, i + 1)
                pe.wait_ge(ab_read, 24 * B + i + 1)
                for c in range(KC):
                    rh = W[:, ds(e, 1), 0, c, :].rearrange("p a n -> p (a n)")
                    rl = W[:, ds(e, 1), 1, c, :].rearrange("p a n -> p (a n)")
                    last = product(ab[:, h, :], st_h[:, h, c, :], st_l[:, h, c, :], rh, rl, c == 0, c == KC - 1)
                last.then_inc(ab_full, 1)

            pe.wait_ge(routed, 1)
            pe.wait_ge(pt_lo, 1 + G)
            turn_rows(0, 0, 0, True)
            for i in range(PEEL):
                turn_rows(i + 1, (i + 1) % 4, (i + 1) // 4, i == 0)
                pe.wait_ge(w_split, 2 * min(i + 1, EARLY))
                if i >= EARLY:
                    pe.wait_ge(w_lo, i + 1 - EARLY)
                expert(i, i % 2)
            with pe.Fori(PEEL // 4, SLOT_TILES // 4 - 1) as i:
                for q in range(4):
                    turn_rows(4 * i + q + 1, (q + 1) % 4, i + (q + 1) // 4)
                    expert(4 * i + q, q % 2)
            for q in range(4):
                if q < 3:
                    turn_rows(SLOT_TILES - 3 + q, q + 1, SLOT_TILES // 4 - 1)
                expert(SLOT_TILES - 4 + q, q % 2)

            def turn_comb(g, q, first=False):
                pe.wait_ge(c_done, g + 1)
                if not first:
                    pe.wait_ge(c_lo, g - 1)
                transpose_tile(comb[:, q, :], q % 2).then_inc(c_t, 1)

            def project(g, h):
                pe.wait_ge(c_lo, g + 1)
                pe.wait_ge(ab_read, 24 * B + SLOT_TILES + g + 1)
                for c in range(KC):
                    last = product(ab[:, h, :], st_h[:, h, c, :], st_l[:, h, c, :],
                                   pw_h[:, c, :], pw_l[:, c, :], c == 0, c == KC - 1)
                last.then_inc(ab_full, 1)

            pe.wait_ge(g_lo, SLOT_TILES)
            pe.wait_ge(w_lo, LATE)
            turn_comb(0, 0, True)
            turn_comb(1, 1, True)
            with pe.Fori(0, G // R - 1) as i:
                for q in range(R):
                    project(R * i + q, q % 2)
                    turn_comb(R * i + q + 2, (q + 2) % R)
            for q in range(R):
                project(G - R + q, q % 2)
                if q + 2 < R:
                    turn_comb(G - R + q + 2, q + 2)

    return None


def kernel(**inputs):
    import numpy as np
    import concourse.bacc as bacc
    from concourse.bass_utils import run_bass_kernel_spmd

    a = {k: np.asarray(v) for k, v in inputs.items()}
    x = a["L0_attn_hidden_states"]
    D = x.shape[-1]
    arrays = {
        "x": x,
        "w_qkv": a["L0_attn_w_qkv"],
        "b_qkv": a["L0_attn_b_qkv"].reshape(3, D // P, P).transpose(2, 0, 1),
        "w_out_t": a["L0_attn_w_out"].T,
        "b_out": a["L0_attn_b_out"],
        "router_w": a["L0_ffn_router_w"],
        "router_b": a["L0_ffn_router_b"],
        "expert_w": a["L0_ffn_expert_w"],
        "expert_b": a["L0_ffn_expert_b"],
        "proj_w": a["L0_ffn_proj_w"],
        "proj_b": a["L0_ffn_proj_b"],
        "norm_w": a["L0_ffn_norm_w"],
    }
    arrays = {f"in_{k}": np.ascontiguousarray(v) for k, v in arrays.items()}
    nc = bacc.Bacc("TRN2", target_bir_lowering=False, num_devices=1)
    args = [nc.dram_tensor(k, v.shape, F32, kind="ExternalInput").ap() for k, v in arrays.items()]
    out = nc.dram_tensor("out", x.shape, F32, kind="ExternalOutput").ap()
    gated_attention_moe(nc, *args, out)
    r = run_bass_kernel_spmd(nc, [arrays], core_ids=[0])
    return r.results[0]["out"]
```

```python
from contextlib import ExitStack

import concourse.bass as bass
from concourse import mybir

P = 128
F32 = mybir.dt.float32
F32R = mybir.dt.float32r
I32 = mybir.dt.int32
ALU = mybir.AluOpType
ACT = mybir.ActivationFunctionType
AX = mybir.AxisListType
ds = bass.ds

LN_EPS = 1e-5
RMS_EPS = 1e-6
RSQRT_SEED = float(0x5F3759DF)


class Chain:

    def __init__(self, eng, sem):
        self.eng, self.sem, self.base, self.k, self.total = eng, sem, 0, 0, 0

    def __call__(self, ins):
        self.k += 1
        ins.then_inc(self.sem, 1)
        self.eng.wait_ge(self.sem, self.base + self.k)

    def enter(self, turn, steps):
        self.total = self.base + self.k
        self.base, self.k, self.steps = self.total + turn * steps, 0, steps

    def leave(self, turns):
        assert self.k == self.steps, (self.k, self.steps)
        self.base, self.k = self.total + turns * self.steps, 0


def gated_attention_moe(nc, x, w_qkv, b_qkv, w_out_t, b_out, router_w, router_b,
                        expert_w, expert_b, proj_w, proj_b, norm_w, out):
    B, S, D = x.shape
    E = router_w.shape[1]
    T = B * S
    KC = D // P
    G = T // P
    GB = S // P
    QB = 4
    NB = GB // QB
    NP = E + 2
    SLOT_TILES = 2 * T // P + E - 1
    R, RY = 4, 8
    SPLITS = (0, 1, 2, E - 1, 3, 4, 5, 6, E)
    EARLY = 4
    SCALE = float(D) ** -0.5
    assert D == KC * P == 512 and GB % QB == 0

    x_v = x.rearrange("b (t p) h -> b p t h", p=P)
    x_g = x.rearrange("b (t p) h -> (b t) p h", p=P)
    out_g = out.rearrange("b (t p) h -> (b t) p h", p=P)
    wqkv_v = w_qkv.rearrange("(w c p) h -> w p c h", w=3, p=P)
    wout_v = w_out_t.rearrange("(c p) n -> p c n", p=P)
    expert_v = expert_w.rearrange("e (c p) f -> e p c f", p=P)
    proj_v = proj_w.rearrange("(c p) f -> p c f", p=P)

    xn_d = nc.dram_tensor("xn_scratch", (T, D), F32).ap()
    s_d = nc.dram_tensor("s_scratch", (T, D), F32).ap()
    y_d = nc.dram_tensor("y_scratch", (SLOT_TILES * P, D), F32).ap()
    tab_d = nc.dram_tensor("slot_token", (SLOT_TILES * P, 1), I32).ap()
    xn_g = xn_d.rearrange("(g p) h -> g p h", p=P)
    s_g = s_d.rearrange("(g p) h -> g p h", p=P)
    y_g = y_d.rearrange("(g p) h -> g p h", p=P)

    with ExitStack() as ctx:
        def sb(name, shape, dt=F32, stack=ctx):
            return stack.enter_context(nc.sbuf_tensor(name, shape, dt))

        def sem(name):
            return ctx.enter_context(nc.semaphore(name))

        def sems(name, n):
            return [sem(f"{name}{i}") for i in range(n)]

        ident = sb("ident", [P, P])
        ones = sb("ones", [P, P])
        tri = sb("tri", [P, P])
        rank8 = sb("rank8", [P, G, E])
        thr = sb("thr", [P, E, G])
        slot_i = sb("slot_i", [P, SLOT_TILES, E])
        ids = sb("ids", [P, G], I32)
        logits = sb("logits", [P, G, NP])
        bcols = sb("bcols", [P, 3, KC])
        tb = sb("tb", [P, KC])
        stats = sb("stats", [P, GB, 6])
        mean = sb("mean", [P, G])
        rstd = sb("rstd", [P, G])
        shift = sb("shift", [P, G])
        small = sb("small", [P, 12, 16])
        rw = sb("rw", [P, KC, NP])
        rw_hl = sb("rw_hl", [P, KC, 2, NP], F32R)
        rb_bc = sb("rb_bc", [P, NP])
        sbias = sb("sbias", [P, D])
        w1 = sb("w1", [P, G])
        w2 = sb("w2", [P, G])
        pos1 = sb("pos1", [P, G], I32)
        pos2 = sb("pos2", [P, G], I32)
        cell1 = sb("cell1", [P, G], I32)
        cell2 = sb("cell2", [P, G], I32)
        token = sb("token", [P, SLOT_TILES], I32)
        texp = sb("texp", [P, SLOT_TILES], I32)
        idx = sb("idx", [P, 8], I32)
        zeros = sb("zeros", [P, SLOT_TILES], I32)
        st_h = sb("st_h", [P, 2, KC, P], F32R)
        st_l = sb("st_l", [P, 2, KC, P], F32R)
        xb = sb("xb", [P, GB, D])
        wraw = xb[:, :, :].rearrange("p (a c) n -> p a c n", a=2)
        xn = sb("xn", [P, 2, D])

        with ExitStack() as a:
            wkeep = sb("wkeep", [P, 2, 2, KC, D], F32R, a)
            nw_h = sb("nw_h", [P, KC, D], F32R, a)
            nw_l = sb("nw_l", [P, KC, D], F32R, a)
            xt_h = sb("xt_h", [P, KC, S], F32R, a)
            xt_l = sb("xt_l", [P, KC, S], F32R, a)
            v_h = sb("v_h", [P, GB, D], F32R, a)
            v_l = sb("v_l", [P, GB, D], F32R, a)
            mw_h = sb("mw_h", [P, KC, D], F32R, a)
            mw_l = sb("mw_l", [P, KC, D], F32R, a)
            t_h = sb("t_h", [P, KC, QB * P], F32R, a)
            t_l = sb("t_l", [P, KC, QB * P], F32R, a)
            pt_h = sb("pt_h", [P, 2, GB, P], F32R, a)
            pt_l = sb("pt_l", [P, 2, GB, P], F32R, a)
            prob = sb("prob", [P, S], F32, a)
            so = sb("so", [P, 2, D], F32, a)
        with ExitStack() as a:
            raw = [sb(f"raw_{n}", [P, KC, D], F32, a) for n in ("q", "k", "v", "o")]
        with ExitStack() as a:
            sb("raw_qk", [P, 2, KC, D], F32, a)
            xb1 = sb("xb1", [P, GB, D], F32, a)
        xbs = (xb, xb1)
        assert B == 2 and GB == 2 * KC
        with ExitStack() as a:
            W = sb("W", [P, E, 2, KC, D], F32R, a)
            bias_e = sb("bias_e", [P, E, D], F32, a)
            pw_h = sb("pw_h", [P, KC, D], F32R, a)
            pw_l = sb("pw_l", [P, KC, D], F32R, a)
            xg = sb("xg", [P, 2, D], F32, a)
            yt = sb("yt", [P, 2, D], F32, a)
        with ExitStack() as a:
            xf = sb("xf", [P, G - R, D], F32, a)
            sf = sb("sf", [P, G - R, D], F32, a)
            yy = sb("yy", [P, G, D], F32, a)
            y1 = sb("y1", [P, RY, D], F32, a)
            y2 = sb("y2", [P, RY, D], F32, a)
            comb = sb("comb", [P, R, D], F32, a)
            nrm_bc = sb("nrm_bc", [P, D], F32, a)
            pb = sb("pb", [1, D], F32, a)
            pb_h = sb("pb_h", [1, D], F32R, a)
            pb_l = sb("pb_l", [1, D], F32R, a)
            one_row = sb("one_row", [1, P], F32R, a)
            sq = sb("sq", [P, 2, D], F32, a)
        x_at = lambda g: xb[:, g, :] if g < R else xf[:, g - R, :]
        s_at = lambda g: xb[:, R + g, :] if g < R else sf[:, g - R, :]
        rows = (xn[:, 0, :], xn[:, 1, :], xg[:, 0, :], xg[:, 1, :])
        bvb = prob[:, 0:KC * P].rearrange("p (c n) -> p c n", c=KC)
        bo_bc = so[:, 0, :]
        prod = so[:, 1, 0:KC]
        wq_h, wq_l = t_h, t_l
        wk_h, wk_l = (v[:, :, :, :].rearrange("p a c n -> p (a c n)").rearrange("p (c n) -> p c n", c=KC)
                      for v in (pt_h, pt_l))
        bias_rows = prob[0:1, 0:2 * D]
        with ExitStack() as a:
            route = sb("route", [P, 10, G, E], F32, a)
            padded = sb("padded", [P, 2, 2 * G, E], F32, a)
            starts = sb("starts", [P, 2, 2 * E], F32, a)
            slots = sb("slots", [P, SLOT_TILES, E], F32, a)

        sc = ctx.enter_context(nc.psum_tensor("sc", [P, 2, 2, 512], F32))
        tp = ctx.enter_context(nc.psum_tensor("tp", [P, 2, KC, P], F32))
        ab = ctx.enter_context(nc.psum_tensor("ab", [P, 2, D], F32))

        vo_in = sems("vo_in", KC)
        qk_in = sems("qk_in", 2)
        vec_in = sem("vec_in")
        rw_in = sem("rw_in")
        x_in = sems("x_in", 2)
        x1_in = sem("x1_in")
        const = sem("const")
        zero_out = sem("zero_out")
        qk_split = sem("qk_split")
        fold = sem("fold")
        fold_h = sem("fold_h")
        fold_l = sem("fold_l")
        pre = sem("pre")
        vecs = sem("vecs")
        rows_out = sem("rows_out")
        pre_done = sem("pre_done")
        dv = sem("dv")
        xn_ready = sem("xn_ready")
        xn_st = sems("xn_st", 2)
        t_done = sem("t_done")
        hi_done = sem("hi_done")
        lo_done = sem("lo_done")
        xh_done = sem("xh_done")
        xl_done = sem("xl_done")
        rt_done = sem("rt_done")
        lt_out = sem("lt_out")
        lt_back = sem("lt_back")
        lg_read = sem("lg_read")
        ab_full = sem("ab_full")
        ab_hi = sem("ab_hi")
        ab_read = sem("ab_read")
        s_done = sem("s_done")
        mx = sem("mx")
        exp_done = sem("exp_done")
        ptr_done = sem("ptr_done")
        pt_hi = sem("pt_hi")
        pt_lo = sem("pt_lo")
        so_st = sems("so_st", 2)
        a_done = sem("a_done")
        cnt = sem("cnt")
        gate_d = sem("gate_d")
        gate_e = sem("gate_e")
        routed = sem("routed")
        pl = sem("pl")
        scat = sem("scat")
        we_in = sems("we_in", 2)
        wr_in = sems("wr_in", 2)
        e_hi = sem("e_hi")
        e_lo = sem("e_lo")
        w_hi = sem("w_hi")
        w_lo = sem("w_lo")
        be_in = sem("be_in")
        ix_in = sem("ix_in")
        xg_in = sems("xg_in", 4)
        g_t = sem("g_t")
        g_hi = sem("g_hi")
        g_lo = sem("g_lo")
        silu_d = sem("silu_d")
        y_st = sems("y_st", 2)
        fin_x = sems("fin_x", G // R)
        fin_s = sems("fin_s", G // R)
        vec2_in = sem("vec2_in")
        pb_hi = sem("pb_hi")
        pb_lo = sem("pb_lo")
        y_in = sems("y_in", RY)
        y1_done = sem("y1_done")
        c_done = sem("c_done")
        c_t = sem("c_t")
        c_hi = sem("c_hi")
        c_lo = sem("c_lo")
        xn_back = sem("xn_back")
        sq_d = sem("sq_d")
        z_done = sem("z_done")
        r_done = sem("r_done")
        r_last = sem("r_last")
        g_done = sem("g_done")
        m_done = sem("m_done")
        o_done = sem("o_done")
        o_dve = sem("o_dve")
        o_st = sem("o_st")
        cnt_read = sem("cnt_read")

        block = ctx.enter_context(nc.Block())
        BY_POOL = 6
        LATE = 2 * (len(SPLITS) - EARLY)
        AHEAD = 4
        RMS = tuple(slice(R * n, R * n + R) for n in range(G // R - 1)) + (slice(G - 4, G - 2), slice(G - 2, G))
        BY_DVE = (G - 5, G - 3, G - 1)
        LAG = 7
        LOOPED = (SLOT_TILES - 1) // 4 * 4
        y_stored = [16 * len(range(h, SLOT_TILES, 2)) for h in range(2)]
        PEEL = E

        def raw_in(k):
            return (we_in[k % 2], 16 * (k // 2 + 1)) if k < BY_POOL else (wr_in[k % 2], 16 * ((k - BY_POOL) // 2 + 1))

        def load_raw(eng, k):
            e = SPLITS[k]
            eng.dma_start(wraw[:, k % 2, :, :], expert_v[e] if e < E else proj_v).then_inc(raw_in(k)[0], 16)

        def halves(m):
            k, c = EARLY + m // 2, slice(m % 2 * KC // 2, (m % 2 + 1) * KC // 2)
            e = SPLITS[k]
            high, low = (W[:, e, 0, c, :], W[:, e, 1, c, :]) if e < E else (pw_h[:, c, :], pw_l[:, c, :])
            return k, wraw[:, k % 2, c, :], high, low

        def rsqrt(eng, link, r, v, t):
            link(eng.tensor_scalar(r.bitcast(I32), v.bitcast(I32), -0.5, RSQRT_SEED, ALU.mult, ALU.add))
            for _ in range(3):
                link(eng.tensor_tensor(t, r, r, ALU.mult))
                link(eng.tensor_tensor(t, t, v, ALU.mult))
                link(eng.tensor_scalar(t, t, -0.5, 1.5, ALU.mult, ALU.add))
                link(eng.tensor_tensor(r, r, t, ALU.mult))

        def group_rms(eng, link, w):
            link(eng.tensor_scalar(small[:, 1, w], small[:, 0, w], 1.0 / D, RMS_EPS, ALU.mult, ALU.add))
            rsqrt(eng, link, small[:, 2, w], small[:, 1, w], small[:, 3, w])

        @block.sync
        def _(sp):
            sp.sem_inc(so_st[0], 16)
            sp.sem_inc(so_st[1], 16)
            for c in range(KC):
                sp.dma_start(raw[2][:, c, :], wqkv_v[2][:, c, :]).then_inc(vo_in[c], 16)
                sp.dma_start(raw[3][:, c, :], wout_v[:, c, :]).then_inc(vo_in[c], 16)
            for h in range(2):
                sp.dma_start(xb[:, h * GB // 2:(h + 1) * GB // 2, :], x_v[0][:, h * GB // 2:(h + 1) * GB // 2, :])\
                    .then_inc(x_in[h], 16)
            for n in (0, 1):
                sp.dma_start(raw[n][:, :, :], wqkv_v[n]).then_inc(qk_in[n], 16)
            for b in range(B):
                with sp.Fori(0, GB // 2) as i:
                    for h in range(2):
                        sp.wait_ge(xn_ready, GB * b + 2 * i + h + 1)
                        sp.dma_start(xn_g[ds(GB * b + 2 * i + h, 1), :, :].rearrange("a p n -> p (a n)"),
                                     xn[:, h, :]).then_inc(xn_st[h], 16)
                    if b == 0:
                        sp.wait_ge(pre_done, 1)
                        sp.dma_start(xb1[:, ds(2 * i, 2), :], x_v[1][:, ds(2 * i, 2), :]).then_inc(x1_in, 16)
                def store_out(i, j):
                    sp.wait_ge(ab_read, 2 + 24 * b + 8 + 8 * i + 4 + j + 1)
                    sp.dma_start(s_g[ds(GB * b + QB * i + j, 1), :, :].rearrange("a p n -> p (a n)"),
                                 so[:, j % 2, :]).then_inc(so_st[j % 2], 16)

                with sp.Fori(0, NB if b + 1 < B else NB - 1) as i:
                    for j in range(QB):
                        store_out(i, j)
            for j in range(QB):
                if j == 1:
                    sp.wait_ge(s_done, G)
                    sp.dma_start(bias_e[:, :, :].rearrange("p e f -> p (e f)"),
                                 expert_b.rearrange("e f -> (e f)").rearrange("(a n) -> a n", a=1)
                                 .to_broadcast([P, E * D])).then_inc(be_in, 16)
                store_out(NB - 1, j)

            def store_y(i, h):
                sp.wait_ge(silu_d, i + 1)
                sp.dma_start(y_g[ds(i, 1), :, :].rearrange("a p n -> p (a n)"), yt[:, h, :])\
                    .then_inc(y_st[h], 16)

            for i in range(PEEL):
                store_y(i, i % 2)
            x_all, s_all = (v.rearrange("g p n -> p g n") for v in (x_g, s_g))
            sp.wait_ge(w_lo, LATE)
            sp.dma_start(xb[:, 0:R, :], x_all[:, 0:R, :]).then_inc(fin_x[0], 16)
            with sp.Fori(PEEL // 2, LOOPED // 2) as i:
                for h in range(2):
                    store_y(2 * i + h, h)
            for i in range(LOOPED, SLOT_TILES):
                store_y(i, i % 2)

            sp.wait_ge(ab_full, 24 * B + SLOT_TILES)
            sp.dma_start(pb[:, :], proj_b.rearrange("(a n) -> a n", a=1)).then_inc(vec2_in, 16)
            sp.dma_start(nrm_bc[:, :], norm_w.rearrange("(a n) -> a n", a=1).to_broadcast([P, D]))\
                .then_inc(vec2_in, 16)
            for q in range(2):
                sp.wait_ge(so_st[q], 16 + 8 * G)
            for n in range(G // R):
                if n + 1 < G // R:
                    w, at = slice(R * n + R, R * n + 2 * R), slice(R * n, R * n + R)
                    sp.wait_ge(c_done, R * n + 1)
                    sp.dma_start(xf[:, at, :], x_all[:, w, :]).then_inc(fin_x[n + 1], 16)
                w = slice(R * n, R * n + R)
                sp.wait_ge(c_done, min(R * n + 3, G))
                sp.dma_start(xb[:, R:2 * R, :] if n == 0 else sf[:, R * n - R:R * n, :], s_all[:, w, :])\
                    .then_inc(fin_s[n], 16)
            for g in range(G):
                mine = [a for a in range(g + 1) if (a in BY_DVE) == (g in BY_DVE)]
                sp.wait_ge(o_dve if g in BY_DVE else o_done, len(mine))
                sp.dma_start(out_g[g], yy[:, g, :]).then_inc(o_st, 16)
            sp.wait_ge(o_st, 16 * G)
            for q in range(2):
                sp.wait_ge(xn_st[q], 8 * G)
                sp.wait_ge(y_st[q], y_stored[q])

        @block.gpsimd
        def _(pool):
            link = Chain(pool, pl)
            pool.memset(ones[:, :], 1.0).then_inc(const, 1)
            link(pool.memset(ident[:, :], 0.0))
            pool.affine_select(out=ident[:, :], in_=ident[:, :], compare_op=ALU.not_equal, fill=1.0,
                               base=0, pattern=[[-1, P]], channel_multiplier=1).then_inc(const, 1)
            pool.wait_ge(const, 1)
            pool.affine_select(out=tri[:, :], in_=ones[:, :], compare_op=ALU.is_gt, fill=0.0,
                               base=0, pattern=[[1, P]], channel_multiplier=-1).then_inc(const, 1)
            pool.iota(rank8[:, :, :], [[0, G], [-1, E]], base=E, channel_multiplier=0,
                      allow_small_or_imprecise_dtypes=True).then_inc(const, 1)
            pool.iota(thr[:, :, :], [[0, E], [P, G]], base=0, channel_multiplier=0,
                      allow_small_or_imprecise_dtypes=True).then_inc(const, 1)
            pool.iota(slot_i[:, :, :], [[1, SLOT_TILES], [0, E]], base=0, channel_multiplier=0,
                      allow_small_or_imprecise_dtypes=True).then_inc(const, 1)
            pool.iota(ids[:, :], [[P, G]], base=0, channel_multiplier=1).then_inc(const, 1)
            link(pool.memset(zeros[:, :], 0))
            pool.dma_start(tab_d.rearrange("(p i) a -> p (i a)", p=P), zeros[:, :]).then_inc(zero_out, 16)
            link(pool.memset(rw[:, :, :], 0.0))
            link(pool.memset(rb_bc[:, :], 0.0))
            pool.dma_start(rw[:, :, 0:E], router_w.rearrange("(c p) e -> p c e", p=P)).then_inc(rw_in, 16)
            pool.dma_start(rb_bc[:, 0:E], router_b.rearrange("(a n) -> a n", a=1).to_broadcast([P, E]))\
                .then_inc(rw_in, 16)
            for n, (high, low) in enumerate(((wq_h, wq_l), (wk_h, wk_l))):
                pool.wait_ge(qk_in[n], 16)
                pool.tensor_copy(high[:, :, :], raw[n][:, :, :]).then_inc(qk_split, 1)
                pool.wait_ge(qk_split, 2 * n + 1)
                pool.tensor_tensor(low[:, :, :], raw[n][:, :, :], high[:, :, :], ALU.subtract).then_inc(qk_split, 1)
            pool.wait_ge(xn_ready, GB)
            for k in range(2):
                load_raw(pool, k)
            pool.wait_ge(routed, 1)
            pool.wait_ge(zero_out, 16)
            for g in range(G):
                for pos in (cell1, cell2):
                    pool.indirect_dma_start(tab_d, bass.IndirectOffsetOnAxis(pos[:, g:g + 1], 0),
                                            ids[:, g:g + 1], None).then_inc(scat, 16)

            def early_low(k):
                e = SPLITS[k]
                pool.wait_ge(e_hi, k + 1)
                pool.tensor_tensor(W[:, e, 1, :, :], wraw[:, k % 2, :, :], W[:, e, 0, :, :], ALU.subtract)\
                    .then_inc(e_lo, 1)
                pool.wait_ge(e_lo, k + 1)
                load_raw(pool, k + 2)

            for k in range(2):
                early_low(k)
            pool.wait_ge(scat, 32 * G)
            pool.dma_start(token[:, :], tab_d.rearrange("(p i) a -> p (i a)", p=P)).then_inc(ix_in, 16)
            early_low(2)

            def gather(i, q):
                link(pool.tensor_copy(idx[:, q:q + 1], token[:, ds(i, 1)]))
                pool.nop(nofuse=True)
                pool.indirect_dma_start(rows[q], None, xn_d,
                                        bass.IndirectOffsetOnAxis(idx[:, q:q + 1], 0)).then_inc(xg_in[q], 16)

            for q in range(2):
                pool.wait_ge(xn_st[q], 8 * G)
            pool.wait_ge(ix_in, 16)
            gather(0, 0)
            gather(1, 1)
            early_low(3)
            pool.wait_ge(ptr_done, 1 + G)
            gather(2, 2)
            gather(3, 3)
            with pool.Fori(0, LOOPED // 4 - 1) as i:
                link.enter(i, 4)
                for q in range(4):
                    pool.wait_ge(g_t, 4 * i + q + 1)
                    gather(4 * i + q + 4, q)
            link.leave(LOOPED // 4 - 1)
            for i in range(LOOPED, SLOT_TILES):
                pool.wait_ge(g_t, i - 3)
                gather(i, i % 4)
            for q in range(2):
                pool.wait_ge(y_st[q], y_stored[q])

            def gather_y(g, q):
                for n, y in enumerate((y1, y2)):
                    pool.indirect_dma_start(y[:, q, :], None, y_d,
                                            bass.IndirectOffsetOnAxis((pos1, pos2)[n][:, g:g + 1], 0))\
                        .then_inc(y_in[q], 16)

            def inverse_rms(n):
                pool.wait_ge(sq_d, RMS[n].stop)
                group_rms(pool, link, RMS[n])
                pool.sem_inc(r_done, 1)

            def add_x(g):
                pool.wait_ge(m_done, g + 1)
                pool.tensor_tensor(yy[:, g, :], yy[:, g, :], x_at(g), ALU.add).then_inc(o_done, 1)

            for g in range(G):
                if g >= RY:
                    pool.wait_ge(c_done, g - RY + 1)
                gather_y(g, g % RY)
                if g == RY + R + 1:
                    inverse_rms(0)
            for g in range(G):
                for n in range(1, len(RMS) - 1):
                    if g == RMS[n].stop - LAG:
                        inverse_rms(n)
                if g not in BY_DVE:
                    add_x(g)

        @block.scalar
        def _(act):
            act.sem_inc(exp_done, 2)
            act.dma_start(bcols[:, :, :], b_qkv).then_inc(vec_in, 16)
            act.dma_start(bo_bc, b_out.rearrange("(a n) -> a n", a=1).to_broadcast([P, D])).then_inc(vec_in, 16)

            def fold_high(n):
                act.wait_ge(fold, n + 1)
                dst = (nw_h if n < KC else mw_h)[:, n % KC, :]
                nc.scalar.copy(dst, sc[:, (n % 4) // 2, n % 2, :]).then_inc(fold_h, 1)

            for n in range(KC):
                fold_high(n)

            for b in range(B):
                def hi(g, t, h):
                    act.wait_ge(t_done, g + 1)
                    nc.scalar.copy(st_h[:, h, :, :], tp[:, h, :, :]).then_inc(hi_done, 1)
                    act.wait_ge(hi_done, g + 1)
                    nc.scalar.copy(xt_h[:, :, ds(t * P, P)], st_h[:, h, :, :]).then_inc(xh_done, 1)

                def v_hi(g, t, h):
                    act.wait_ge(ab_full, 24 * b + t + 1)
                    nc.scalar.copy(v_h[:, ds(t, 1), :].rearrange("p a n -> p (a n)"), ab[:, h, :]).then_inc(ab_hi, 1)

                g0 = GB * b
                hi(g0, 0, 0)
                hi(g0 + 1, 1, 1)
                with act.Fori(0, GB // 2 - 1) as i:
                    for h in range(2):
                        v_hi(g0 + 2 * i + h, 2 * i + h, h)
                        hi(g0 + 2 * i + h + 2, 2 * i + h + 2, h)
                for h in range(2):
                    v_hi(g0 + GB - 2 + h, GB - 2 + h, h)

                if b == 0:
                    act.wait_ge(vecs, 2)
                    nc.scalar.copy(bias_rows, ab[0:1, :, :].rearrange("p a n -> p (a n)")).then_inc(rows_out, 1)
                    for n in range(KC, 2 * KC):
                        fold_high(n)
                act.wait_ge(rt_done, b + 1)
                nc.scalar.copy(prob[0:2 * NP, :], tp[0:2 * NP, :, :, :].rearrange("p a c n -> p (a c n)"))\
                    .then_inc(lt_out, 1)

                def early_high(k):
                    e = SPLITS[k]
                    act.wait_ge(routed, 1)
                    act.wait_ge(*raw_in(k))
                    nc.scalar.copy(W[:, e, 0, :, :], wraw[:, k % 2, :, :]).then_inc(e_hi, 1)

                def attention_block(i, route_here=False, tail=False):
                    for c in range(KC):
                        act.wait_ge(ab_full, 24 * b + 8 + 8 * i + c + 1)
                        nc.scalar.activation(t_h[:, c, :], ab[:, c % 2, :], ACT.Identity, bias=tb[:, c:c + 1])\
                            .then_inc(ab_hi, 1)

                    def pt_split(j):
                        act.wait_ge(ptr_done, 1 + g0 + QB * i + j + 1)
                        nc.scalar.copy(pt_h[:, j % 2, :, :], tp[:, :, :, :].rearrange("p a c n -> p (a c) n"))\
                            .then_inc(pt_hi, 1)

                    for j in range(QB):
                        if j >= 1:
                            pt_split(j - 1)
                        if tail:
                            early_high(j)
                        act.wait_ge(mx, g0 + QB * i + j + 1)
                        act.wait_ge(ptr_done, g0 + QB * i + j + 1)
                        nc.scalar.activation(prob[:, :], sc[:, j % 2, :, :].rearrange("p a n -> p (a n)"), ACT.Exp,
                                             bias=small[:, 4 + j, 1:2], scale=SCALE,
                                             accum_out=small[:, 4 + j, 2:3]).then_inc(exp_done, 1)
                        if route_here and j == 0:
                            act.wait_ge(gate_d, 1)
                            nc.scalar.activation(small[:, 10, :], small[:, 9, :], ACT.Exp).then_inc(gate_e, 1)
                    pt_split(QB - 1)

                if b + 1 < B:
                    with act.Fori(0, NB) as i:
                        attention_block(i)
                else:
                    attention_block(0, True)
                    for i in range(1, NB):
                        attention_block(i, tail=i == NB - 1)

            def g_split(i, h):
                act.wait_ge(g_t, i + 1)
                nc.scalar.copy(st_h[:, h, :, :], tp[:, h, :, :]).then_inc(g_hi, 1)

            def silu(i, h):
                act.wait_ge(ab_read, 2 + 24 * B + i + 1)
                nc.scalar.activation(yt[:, h, :], yt[:, h, :], ACT.Silu).then_inc(silu_d, 1)

            def w_high(m):
                k, whole, high, _ = halves(m)
                act.wait_ge(*raw_in(k))
                nc.scalar.copy(high, whole).then_inc(w_hi, 1)

            def load_next(k):
                act.wait_ge(w_lo, 2 * (k - 1 - EARLY))
                load_raw(act, k)

            act.wait_ge(s_done, G)
            for m in range(AHEAD):
                w_high(m)
                if m == 1:
                    load_next(BY_POOL)
                    g_split(0, 0)
            act.wait_ge(ab_full, 24 * B)
            for i in range(PEEL):
                g_split(i + 1, (i + 1) % 2)
                if 1 <= i <= LATE - AHEAD:
                    w_high(i + AHEAD - 1)
                silu(i, i % 2)
                if i in (0, 2):
                    load_next(BY_POOL + 1 + i // 2)
            with act.Fori(PEEL // 2, LOOPED // 2) as i:
                for h in range(2):
                    g_split(2 * i + h + 1, 1 - h)
                    silu(2 * i + h, h)
            for i in range(LOOPED, SLOT_TILES):
                if i + 1 < SLOT_TILES:
                    g_split(i + 1, (i + 1) % 2)
                silu(i, i % 2)

            def scale(g):
                q = g % RY
                act.wait_ge(y_in[q], 32 * (g // RY + 1))
                nc.scalar.mul(y1[:, q, :], y1[:, q, :], w1[:, g:g + 1]).then_inc(y1_done, 1)

            def normalise(g):
                act.wait_ge(fin_x[g // R], 16)
                nc.scalar.activation(yy[:, g, :], x_at(g), ACT.Identity, bias=shift[:, g:g + 1],
                                     scale=rstd[:, g:g + 1]).then_inc(xn_back, 1)

            def c_split(g):
                act.wait_ge(c_t, g + 1)
                nc.scalar.copy(st_h[:, g % 2, :, :], tp[:, g % 2, :, :]).then_inc(c_hi, 1)

            def squares(g):
                act.wait_ge(ab_read, 2 + 24 * B + SLOT_TILES + g + 1)
                nc.scalar.activation(sq[:, g % 2, :], yy[:, g, :], ACT.Square,
                                     accum_out=small[:, 0, g:g + 1]).then_inc(sq_d, 1)

            def gate(g):
                if g < RMS[-1].start:
                    act.wait_ge(r_done, 1 + [w.start <= g < w.stop for w in RMS].index(True))
                else:
                    act.wait_ge(r_last, 1)
                act.wait_ge(z_done, g + 1)
                nc.scalar.activation(yy[:, g, :], yy[:, g, :], ACT.Silu, scale=small[:, 2, g:g + 1])\
                    .then_inc(g_done, 1)

            act.wait_ge(vec2_in, 32)
            nc.scalar.copy(pb_h[:, :], pb[:, :]).then_inc(pb_hi, 1)
            for step in range(-2, G + LAG):
                for lag, do in ((0, c_split), (-2, scale), (-2, normalise), (LAG - 1, gate), (1, squares)):
                    if 0 <= step - lag < G:
                        do(step - lag)

        @block.vector
        def _(dve):
            link = Chain(dve, dv)
            vec = nc.vector

            dve.sem_inc(ab_read, 2)
            dve.sem_inc(pt_lo, 1)
            dve.wait_ge(vec_in, 32)
            dve.wait_ge(const, 1)
            vec.tensor_tensor(prod, bcols[:, 0, :], bcols[:, 1, :], ALU.mult).then_inc(pre, 1)
            for c in range(KC):
                vec.tensor_scalar(bvb[:, c, :], ones[:, :], bcols[:, 2, c:c + 1], None, ALU.mult).then_inc(pre, 1)

            def row_stats(b):
                for t in range(GB):
                    if t % (GB // 2) == 0:
                        dve.wait_ge(*((x1_in, 8 * GB) if b else (x_in[t // (GB // 2)], 16)))
                    last = vec.bn_stats(stats[:, t, :], xbs[b][:, t, :])
                link(last)

            def batch_stats(b):
                g0 = GB * b
                me, mo = stats[:, :, 1], stats[:, :, 4]
                ve, vo = stats[:, :, 2], stats[:, :, 5]
                m, r = mean[:, g0:g0 + GB], rstd[:, g0:g0 + GB]
                a, v = small[:, 0, 0:GB], small[:, 1, 0:GB]
                link(vec.tensor_tensor(a, me, mo, ALU.subtract))
                link(vec.tensor_tensor(a, a, a, ALU.mult))
                link(vec.tensor_tensor(v, ve, vo, ALU.add))
                link(vec.tensor_scalar(a, a, 0.25, LN_EPS, ALU.mult, ALU.add))
                link(vec.scalar_tensor_tensor(v, v, 1.0 / D, a, ALU.mult, ALU.add))
                link(vec.tensor_tensor(m, me, mo, ALU.add))
                link(vec.tensor_scalar(m, m, 0.5, None, ALU.mult))
                rsqrt(vec, link, r, v, a)
                link(vec.scalar_tensor_tensor(shift[:, g0:g0 + GB], m, -1.0, r, ALU.mult, ALU.mult))

            def normalise(b, t, h, first=False):
                g = GB * b + t
                if not first:
                    dve.wait_ge(t_done, g - 1)
                    dve.wait_ge(xn_st[h], 8 * (g - h))
                vec.tensor_scalar(xn[:, h, :], xbs[b][:, ds(t, 1), :].rearrange("p a n -> p (a n)"),
                                  mean[:, ds(g, 1)], rstd[:, ds(g, 1)], ALU.subtract, ALU.mult).then_inc(xn_ready, 1)

            def lo(b, t, h):
                g = GB * b + t
                dve.wait_ge(hi_done, g + 1)
                vec.tensor_tensor(st_l[:, h, :, :], tp[:, h, :, :], st_h[:, h, :, :], ALU.subtract).then_inc(lo_done, 1)
                dve.wait_ge(lo_done, g + 1)
                vec.tensor_copy(xt_l[:, :, ds(t * P, P)], st_l[:, h, :, :]).then_inc(xl_done, 1)

            def read_logits(b):
                dve.wait_ge(lt_back, b + 1)
                two = tp[:, 0, :, :].rearrange("p c n -> p (c n)")[:, 0:GB * 2 * NP]
                L = logits[:, GB * b:GB * (b + 1), :]
                link(vec.tensor_reduce(L, two.rearrange("p (t a n) -> p t n a", t=GB, a=2), AX.X, ALU.add))
                link(vec.tensor_tensor(L, L, rb_bc[:, :].unsqueeze(1).to_broadcast([P, GB, NP]), ALU.add))
                dve.sem_inc(lg_read, 1)

            def v_lo(b, t, h):
                dve.wait_ge(ab_hi, 16 * b + t + 1)
                vec.tensor_tensor(v_l[:, ds(t, 1), :].rearrange("p a n -> p (a n)"), ab[:, h, :],
                                  v_h[:, ds(t, 1), :].rearrange("p a n -> p (a n)"), ALU.subtract).then_inc(ab_read, 1)

            def fold_low(n):
                dve.wait_ge(fold_h, n + 1)
                h, l = (nw_h, nw_l) if n < KC else (mw_h, mw_l)
                vec.tensor_tensor(l[:, n % KC, :], sc[:, (n % 4) // 2, n % 2, :], h[:, n % KC, :], ALU.subtract)\
                    .then_inc(fold_l, 1)

            def fold_value_bias():
                dve.wait_ge(vecs, 1)
                vec.tensor_tensor(sbias[:, :], ab[:, 1, :], bo_bc, ALU.add).then_inc(pre_done, 1)

            def fold_biases():
                dve.wait_ge(rw_in, 32)
                dve.wait_ge(const, 7)
                dve.wait_ge(vecs, 3)
                vec.tensor_copy(tb[:, :], ab[:, 0, 0:KC]).then_inc(pre_done, 1)
                link(vec.tensor_copy(rw[:, :, E], ab[:, 0, KC:2 * KC]))
                vec.tensor_reduce(rb_bc[:, E:E + 1], ab[:, 0, 2 * KC:3 * KC], AX.X, ALU.add).then_inc(pre_done, 1)
                link(vec.tensor_copy(rw_hl[:, :, 0, :], rw[:, :, :]))
                vec.tensor_tensor(rw_hl[:, :, 1, :], rw[:, :, :], rw_hl[:, :, 0, :], ALU.subtract).then_inc(pre_done, 1)
                dve.wait_ge(pre_done, 4)

            def choose():
                L = logits[:, :, 0:E]
                row = lambda n: small[:, n, :]
                wide = lambda n: route[:, n, :, :]
                per_token = lambda v: v.unsqueeze(2).to_broadcast([P, G, E])

                def best(values, top, last, onehot):
                    link(vec.tensor_reduce(top, values, AX.X, ALU.max))
                    link(vec.tensor_tensor(wide(0), values, per_token(top), ALU.is_equal))
                    link(vec.tensor_tensor(wide(0), wide(0), rank8[:, :, :], ALU.mult))
                    link(vec.tensor_reduce(last, wide(0), AX.X, ALU.max))
                    link(vec.tensor_tensor(onehot, rank8[:, :, :], per_token(last), ALU.is_equal))

                best(L, row(0), row(1), wide(1))
                link(vec.scalar_tensor_tensor(wide(2), wide(1), -3e38, L, ALU.mult, ALU.add))
                best(wide(2), row(2), row(1), wide(3))
                vec.tensor_tensor(wide(4), wide(1), wide(3), ALU.add).then_inc(a_done, 1)
                vec.tensor_tensor(row(9), row(2), row(0), ALU.subtract).then_inc(gate_d, 1)
                link(vec.memset(padded[:, :, :, :], 0.0))
                link(vec.memset(starts[:, :, :], 0.0))
                yield
                dve.wait_ge(cnt, 1)
                for n, m in ((5, 0), (6, 1)):
                    count = tp[:, m, :, :].rearrange("p c n -> p (c n)")[:, 0:G * E]
                    link(vec.tensor_copy(wide(n), count.rearrange("p (g e) -> p g e", e=E)))
                vec.tensor_copy(padded[:, 0, G:2 * G, :], wide(6)).then_inc(cnt_read, 1)
                dve.wait_ge(cnt_read, 1)
                src, back = 0, 1
                while back < G:
                    link(vec.tensor_tensor(padded[:, 1 - src, G:2 * G, :], padded[:, src, G:2 * G, :],
                                           padded[:, src, G - back:2 * G - back, :], ALU.add))
                    src, back = 1 - src, 2 * back
                link(vec.tensor_tensor(wide(7), padded[:, src, G:2 * G, :], wide(6), ALU.subtract))
                yield
                dve.wait_ge(gate_e, 1)
                link(vec.tensor_scalar(row(11), row(10), 1.0, None, ALU.add))
                link(vec.reciprocal(w1[:, :], row(11)))
                link(vec.tensor_tensor(w2[:, :], w1[:, :], row(10), ALU.mult))
                total = padded[:, src, 2 * G - 1, :]
                by_tile = wide(8).rearrange("p g e -> p (g e)").rearrange("p (e g) -> p e g", e=E)
                link(vec.scalar_tensor_tensor(by_tile, total.unsqueeze(2).to_broadcast([P, E, G]), 1.0, thr[:, :, :],
                                              ALU.max, ALU.is_gt))
                n_tiles, first = small[:, 8, 0:E], small[:, 11, 0:E]
                link(vec.tensor_reduce(n_tiles, by_tile, AX.X, ALU.add))
                link(vec.tensor_copy(starts[:, 0, E:2 * E], n_tiles))
                src, back = 0, 1
                while back < E:
                    link(vec.tensor_tensor(starts[:, 1 - src, E:2 * E], starts[:, src, E:2 * E],
                                           starts[:, src, E - back:2 * E - back], ALU.add))
                    src, back = 1 - src, 2 * back
                link(vec.tensor_tensor(first, starts[:, src, E:2 * E], n_tiles, ALU.subtract))
                yield
                link(vec.tensor_tensor(slots[:, :, :], slot_i[:, :, :],
                                       first.unsqueeze(1).to_broadcast([P, SLOT_TILES, E]), ALU.is_ge))
                of_tile = wide(9).rearrange("p g e -> p (g e)")[:, 0:SLOT_TILES]
                link(vec.tensor_reduce(of_tile, slots[:, :, :], AX.X, ALU.add))
                link(vec.tensor_scalar(texp[:, :], of_tile, -1.0, None, ALU.add))
                yield
                link(vec.scalar_tensor_tensor(wide(7), first.unsqueeze(1).to_broadcast([P, G, E]), float(P), wide(7),
                                              ALU.mult, ALU.add))
                link(vec.tensor_tensor(wide(7), wide(7), wide(5), ALU.add))
                for onehot, pos in ((wide(1), pos1), (wide(3), pos2)):
                    link(vec.tensor_tensor(wide(8), wide(7), onehot, ALU.mult))
                    link(vec.tensor_reduce(row(1), wide(8), AX.X, ALU.add))
                    link(vec.tensor_copy(pos[:, :], row(1)))
                    at, cell = row(2).bitcast(I32), (cell1 if pos is pos1 else cell2)
                    link(vec.tensor_scalar(at, pos[:, :], P - 1, None, ALU.bitwise_and))
                    link(vec.tensor_scalar(cell[:, :], pos[:, :], P.bit_length() - 1, None, ALU.logical_shift_right))
                    link(vec.scalar_tensor_tensor(cell[:, :], at, float(SLOT_TILES), cell[:, :], ALU.mult, ALU.add))
                dve.sem_inc(routed, 1)

            def g_low(i, h):
                dve.wait_ge(g_hi, i + 1)
                vec.tensor_tensor(st_l[:, h, :, :], tp[:, h, :, :], st_h[:, h, :, :], ALU.subtract).then_inc(g_lo, 1)

            def w_low(m):
                _, whole, high, low = halves(m)
                dve.wait_ge(w_hi, m + 1)
                vec.tensor_tensor(low, whole, high, ALU.subtract).then_inc(w_lo, 1)

            row_stats(0)
            batch_stats(0)
            normalise(0, 0, 0, True)
            normalise(0, 1, 1, True)
            for n in range(KC):
                fold_low(n)
            fold_value_bias()
            for b in range(B):
                g0 = GB * b
                lo(b, 0, 0)
                with dve.Fori(0, GB // 2 - 1) as i:
                    for h in range(2):
                        t = 2 * i + h
                        normalise(b, t + 2, h)
                        lo(b, t + 1, 1 - h)
                        v_lo(b, t, h)
                lo(b, GB - 1, 1)
                for h in range(2):
                    v_lo(b, GB - 2 + h, h)

                if b + 1 < B:
                    row_stats(b + 1)
                    fold_low(KC)
                    fold_low(KC + 1)
                    fold_biases()
                    batch_stats(b + 1)
                    fold_low(KC + 2)
                    normalise(b + 1, 0, 0)
                    normalise(b + 1, 1, 1)
                    fold_low(KC + 3)
                    read_logits(b)

                def attention_block(i, routing=None, tail=False):
                    def go_on():
                        if routing:
                            next(routing, None)

                    for c in range(KC):
                        dve.wait_ge(ab_hi, 16 * b + 8 + KC * i + c + 1)
                        vec.scalar_tensor_tensor(t_l[:, c, :], ab[:, c % 2, :], tb[:, c:c + 1], t_h[:, c, :],
                                                 ALU.add, ALU.subtract).then_inc(ab_read, 1)
                        if routing and c == 0:
                            read_logits(b)
                    go_on()

                    def row_max(j):
                        n = g0 + QB * i + j
                        key = logits[:, ds(n, 1), E:E + 1].rearrange("p a n -> p (a n)")
                        dve.wait_ge(s_done, n + 1)
                        link(vec.tensor_reduce(small[:, 4 + j, 0:1], sc[:, j % 2, :, :], AX.XY, ALU.max, negate=True))
                        link(vec.tensor_tensor(small[:, 4 + j, 1:2], small[:, 4 + j, 0:1], key, ALU.subtract))
                        vec.tensor_scalar(small[:, 4 + j, 1:2], small[:, 4 + j, 1:2], key, SCALE, ALU.add, ALU.mult)\
                            .then_inc(mx, 1)

                    def pt_low(j):
                        dve.wait_ge(pt_hi, g0 + QB * i + j + 1)
                        vec.tensor_tensor(pt_l[:, j % 2, :, :], tp[:, :, :, :].rearrange("p a c n -> p (a c) n"),
                                          pt_h[:, j % 2, :, :], ALU.subtract).then_inc(pt_lo, 1)

                    def attn_out(j):
                        dve.wait_ge(ab_full, 24 * b + 8 + 8 * i + 4 + j + 1)
                        link(vec.reciprocal(small[:, 4 + j, 3:4], small[:, 4 + j, 2:3]))
                        dve.wait_ge(so_st[j % 2], 8 * g0 + 32 * i + 16 * (j // 2) + 16)
                        vec.scalar_tensor_tensor(so[:, j % 2, :], ab[:, j % 2, :], small[:, 4 + j, 3:4], sbias[:, :],
                                                 ALU.mult, ALU.add).then_inc(ab_read, 1)

                    row_max(0)
                    go_on()
                    row_max(1)
                    go_on()
                    pt_low(0)
                    row_max(2)
                    go_on()
                    pt_low(1)
                    attn_out(0)
                    row_max(3)
                    go_on()
                    pt_low(2)
                    attn_out(1)
                    pt_low(3)
                    if tail:
                        w_low(0)
                        w_low(1)
                    attn_out(2)
                    if tail:
                        g_low(0, 0)
                        w_low(2)
                        w_low(3)
                    attn_out(3)

                if b + 1 < B:
                    with dve.Fori(0, NB) as i:
                        link.enter(i, 3 * QB)
                        attention_block(i)
                    link.leave(NB)
                else:
                    attention_block(0, routing=choose())
                    for i in range(1, NB):
                        attention_block(i, tail=i == NB - 1)

            def add_bias(i, h, first=False):
                e = dve.value_load(texp[0:1, ds(i, 1)], min_val=0, max_val=E - 1)
                dve.wait_ge(ab_full, 24 * B + i + 1)
                if not first:
                    dve.wait_ge(y_st[h], 8 * (i - h))
                vec.tensor_tensor(yt[:, h, :], ab[:, h, :], bias_e[:, ds(e, 1), :].rearrange("p a n -> p (a n)"),
                                  ALU.add).then_inc(ab_read, 1)

            for i in range(PEEL):
                g_low(i + 1, (i + 1) % 2)
                if i < 2:
                    dve.wait_ge(so_st[i], 16 + 8 * G)
                    dve.wait_ge(be_in, 16)
                add_bias(i, i % 2, i < 2)
                if 1 <= i <= LATE - AHEAD:
                    w_low(i + AHEAD - 1)
            with dve.Fori(PEEL // 2, LOOPED // 2) as i:
                for h in range(2):
                    g_low(2 * i + h + 1, 1 - h)
                    add_bias(2 * i + h, h)
            for i in range(LOOPED, SLOT_TILES):
                if i + 1 < SLOT_TILES:
                    g_low(i + 1, (i + 1) % 2)
                add_bias(i, i % 2)

            def combine(g):
                q = g % RY
                dve.wait_ge(y1_done, g + 1)
                vec.scalar_tensor_tensor(comb[:, g % R, :], y2[:, q, :], w2[:, g:g + 1], y1[:, q, :],
                                         ALU.mult, ALU.add).then_inc(c_done, 1)

            def c_low(g):
                dve.wait_ge(c_hi, g + 1)
                vec.tensor_tensor(st_l[:, g % 2, :, :], tp[:, g % 2, :, :], st_h[:, g % 2, :, :], ALU.subtract)\
                    .then_inc(c_lo, 1)

            def add_product(g):
                dve.wait_ge(xn_back, g + 1)
                dve.wait_ge(ab_full, 24 * B + SLOT_TILES + g + 1)
                vec.tensor_tensor(yy[:, g, :], ab[:, (SLOT_TILES + g) % 2, :], yy[:, g, :], ALU.add).then_inc(ab_read, 1)

            def weigh(g):
                dve.wait_ge(sq_d, g + 1)
                vec.tensor_tensor(yy[:, g, :], yy[:, g, :], nrm_bc[:, :], ALU.mult).then_inc(z_done, 1)

            def times_s(g):
                dve.wait_ge(fin_s[g // R], 16)
                dve.wait_ge(g_done, g + 1)
                vec.tensor_tensor(yy[:, g, :], yy[:, g, :], s_at(g), ALU.mult).then_inc(m_done, 1)
                if g in BY_DVE:
                    dve.wait_ge(m_done, g + 1)
                    vec.tensor_tensor(yy[:, g, :], yy[:, g, :], x_at(g), ALU.add).then_inc(o_dve, 1)

            dve.wait_ge(pb_hi, 1)
            vec.tensor_tensor(pb_l[:, :], pb[:, :], pb_h[:, :], ALU.subtract).then_inc(pb_lo, 1)
            vec.tensor_copy(one_row[:, :], ones[0:1, :]).then_inc(pb_lo, 1)
            for step in range(-1, G + LAG):
                for lag, do in ((-1, combine), (0, c_low), (1, add_product), (LAG, times_s), (2, weigh)):
                    if 0 <= step - lag < G:
                        do(step - lag)
                if step == G + 1:
                    dve.wait_ge(sq_d, G)
                    group_rms(vec, link, RMS[-1])
                    dve.sem_inc(r_last, 1)

        @block.tensor
        def _(pe):
            def product(dst, lh, ll, rh, rl, start, stop):
                nc.tensor.matmul(dst, lh, rh, start=start, stop=False)
                nc.tensor.matmul(dst, lh, rl, start=False, stop=False)
                return nc.tensor.matmul(dst, ll, rh, start=False, stop=stop)

            def transpose_tile(src, h):
                for c in range(KC):
                    last = nc.tensor.transpose(tp[:, h, c, :], src[:, c * P:(c + 1) * P], ident[:, :])
                return last

            pe.sem_inc(ptr_done, 1)
            def turn_rows(i, q, j, first=False):
                pe.wait_ge(xg_in[q], 16 * (j + 1))
                if not first:
                    pe.wait_ge(g_lo, i - 1)
                transpose_tile(rows[q], q % 2).then_inc(g_t, 1)

            for c in range(KC):
                pe.wait_ge(vo_in[c], 32)
                for n in range(KC):
                    last = nc.tensor.matmul(sc[:, n // 2, n % 2, :], raw[2][:, c, n * P:(n + 1) * P], raw[3][:, c, :],
                                            start=(c == 0), stop=(c == KC - 1))
                    if c == KC - 1:
                        last.then_inc(fold, 1)
            pe.wait_ge(pre, 1 + KC)
            for c in range(KC):
                last = nc.tensor.matmul(ab[:, 1, :], bvb[:, c, :], raw[3][:, c, :], start=(c == 0), stop=(c == KC - 1))
            last.then_inc(vecs, 1)

            def bias_products():
                for m, right in enumerate((raw[1], raw[0])):
                    for c in range(KC):
                        last = nc.tensor.matmul(ab[0:1, m, :], bcols[:, m, c:c + 1], right[:, c, :],
                                                start=(c == 0), stop=(c == KC - 1))
                last.then_inc(vecs, 1)

            def turn_biases():
                pe.wait_ge(rows_out, 1)
                for n in range(2 * KC):
                    nc.tensor.transpose(ab[:, 0, n:n + 1], bias_rows[:, n * P:(n + 1) * P], ident[0:1, 0:1])
                nc.tensor.matmul(ab[:, 0, 2 * KC:3 * KC], ones[:, :], prod, start=True, stop=True).then_inc(vecs, 1)

            for b in range(B):
                g0 = GB * b

                def turn(g, h, first=False):
                    pe.wait_ge(xn_ready, g + 1)
                    if not first:
                        pe.wait_ge(lo_done, g - 1)
                    transpose_tile(xn[:, h, :], h).then_inc(t_done, 1)

                def tile_product(g, t, h):
                    pe.wait_ge(lo_done, g + 1)
                    pe.wait_ge(ab_read, 24 * b + t + 1)
                    for c in range(KC):
                        last = product(ab[:, h, :], st_h[:, h, c, :], st_l[:, h, c, :],
                                       nw_h[:, c, :], nw_l[:, c, :], c == 0, c == KC - 1)
                    last.then_inc(ab_full, 1)

                if b:
                    pe.wait_ge(pt_lo, 1 + g0)
                else:
                    pe.wait_ge(const, 7)
                turn(g0, 0, b == 0)
                if b == 0:
                    pe.wait_ge(fold_l, KC)
                    pe.wait_ge(pre_done, 1)
                for h in range(2):
                    turn(g0 + h + 1, 1 - h, b == 0 and h == 0)
                    tile_product(g0 + h, h, h)
                with pe.Fori(1, GB // 2 - 1) as i:
                    for h in range(2):
                        turn(g0 + 2 * i + h + 1, 1 - h)
                        tile_product(g0 + 2 * i + h, 2 * i + h, h)
                turn(g0 + GB - 1, 1)
                for h in range(2):
                    tile_product(g0 + GB - 2 + h, GB - 2 + h, h)

                pe.wait_ge(ab_read, 2 + 24 * b + GB)
                if b == 0:
                    for n in range(2):
                        pe.wait_ge(qk_in[n], 16)
                    bias_products()
                    pe.wait_ge(qk_split, 4)
                    for n in range(KC):
                        for c in range(KC):
                            w = slice(n * P, (n + 1) * P)
                            last = product(sc[:, n // 2, n % 2, :], wq_h[:, c, w], wq_l[:, c, w],
                                           wk_h[:, c, :], wk_l[:, c, :], c == 0, c == KC - 1)
                        last.then_inc(fold, 1)
                        if n == 1:
                            turn_biases()
                    pe.wait_ge(pre_done, 4)
                pe.wait_ge(lo_done, g0 + GB)
                pe.wait_ge(xh_done, g0 + GB)
                pe.wait_ge(xl_done, g0 + GB)
                for m in range(2):
                    keys = slice(m * 512, (m + 1) * 512)
                    logits_t = tp[:, m, :, :].rearrange("p c n -> p (c n)")
                    for c in range(KC):
                        both = rw_hl[:, c, :, :].rearrange("p a n -> p (a n)")
                        last = nc.tensor.matmul(logits_t[0:2 * NP, :], both, xt_h[:, c, keys], start=(c == 0),
                                                stop=(c == KC - 1))
                        if c + 1 < KC:
                            nc.tensor.matmul(logits_t[0:NP, :], rw_hl[:, c, 0, :], xt_l[:, c, keys],
                                             start=False, stop=False)
                        if c + 2 == KC:
                            nc.tensor.matmul(logits_t[0:NP, :], rw_hl[:, KC - 1, 0, :], xt_l[:, KC - 1, keys],
                                             start=False, stop=False)
                last.then_inc(rt_done, 1)

                def turn_logits():
                    pe.wait_ge(lt_out, b + 1)
                    for t in range(GB):
                        last = nc.tensor.transpose(tp[:, 0, :, :].rearrange("p c n -> p (c n)")[:, 2 * NP * t:2 * NP * (t + 1)],
                                                   prob[0:2 * NP, t * P:(t + 1) * P], ident[0:2 * NP, 0:2 * NP])
                    last.then_inc(lt_back, 1)

                if b == 0:
                    turn_logits()
                    pe.wait_ge(fold_l, 2 * KC)

                def count_chosen():
                    pe.wait_ge(a_done, 1)
                    chosen = route[:, 4, :, :].rearrange("p g e -> p (g e)")
                    for m, w in enumerate((tri, ones)):
                        dst = tp[:, m, :, :].rearrange("p c n -> p (c n)")[:, 0:G * E]
                        last = nc.tensor.matmul(dst, w[:, :], chosen, start=True, stop=True)
                    last.then_inc(cnt, 1)

                def attention_block(i, route_here=False, tail=False):
                    use = 24 * b + 8 + 8 * i

                    def scores(j):
                        a = g0 + QB * i + j
                        pe.wait_ge(exp_done, a + 1)
                        for c in range(KC):
                            if j == 0:
                                pe.wait_ge(ab_read, use + 2 + c + 1)
                            for m in range(2):
                                last = product(sc[:, j % 2, m, :], t_h[:, c, j * P:(j + 1) * P],
                                               t_l[:, c, j * P:(j + 1) * P],
                                               xt_h[:, c, m * 512:(m + 1) * 512], xt_l[:, c, m * 512:(m + 1) * 512],
                                               c == 0, c == KC - 1)
                        last.then_inc(s_done, 1)

                    def turn_probs(j):
                        a = g0 + QB * i + j
                        pe.wait_ge(exp_done, a + 3)
                        pe.wait_ge(pt_lo, a + 1)
                        transpose_tile(prob[:, 0:KC * P], 0)
                        transpose_tile(prob[:, KC * P:2 * KC * P], 1).then_inc(ptr_done, 1)

                    def attend(j):
                        a = g0 + QB * i + j
                        pe.wait_ge(pt_lo, a + 2)
                        pe.wait_ge(ab_read, use + KC + j + 1)
                        for c in range(GB):
                            last = product(ab[:, j % 2, :], pt_h[:, j % 2, c, :], pt_l[:, j % 2, c, :],
                                           v_h[:, c, :], v_l[:, c, :], c == 0, c == GB - 1)
                        last.then_inc(ab_full, 1)

                    for n in range(KC):
                        pe.wait_ge(ab_read, use + n + 1)
                        for c in range(KC):
                            w = slice(n * P, (n + 1) * P)
                            q = ds(i * (QB * P), QB * P)
                            last = product(ab[:, n % 2, :], mw_h[:, c, w], mw_l[:, c, w], xt_h[:, c, q], xt_l[:, c, q],
                                           c == 0, c == KC - 1)
                        last.then_inc(ab_full, 1)
                        if route_here and n == 0:
                            turn_logits()
                    scores(0)
                    if route_here:
                        count_chosen()
                    scores(1)
                    pe.wait_ge(lg_read, b + 1)
                    if route_here:
                        pe.wait_ge(cnt_read, 1)
                    turn_probs(0)
                    scores(2)
                    turn_probs(1)
                    attend(0)
                    scores(3)
                    turn_probs(2)
                    attend(1)
                    turn_probs(3)
                    attend(2)
                    if tail:
                        pe.wait_ge(pt_lo, 1 + G)
                        turn_rows(0, 0, 0, True)
                    attend(3)

                if b + 1 < B:
                    with pe.Fori(0, NB) as i:
                        attention_block(i)
                else:
                    attention_block(0, True)
                    for i in range(1, NB):
                        attention_block(i, tail=i == NB - 1)

            def expert(i, h):
                e = pe.value_load(texp[0:1, ds(i, 1)], min_val=0, max_val=E - 1)
                pe.wait_ge(g_lo, i + 1)
                pe.wait_ge(ab_read, 24 * B + i + 1)
                for c in range(KC):
                    rh = W[:, ds(e, 1), 0, c, :].rearrange("p a n -> p (a n)")
                    rl = W[:, ds(e, 1), 1, c, :].rearrange("p a n -> p (a n)")
                    last = product(ab[:, h, :], st_h[:, h, c, :], st_l[:, h, c, :], rh, rl, c == 0, c == KC - 1)
                last.then_inc(ab_full, 1)

            pe.wait_ge(routed, 1)
            for i in range(PEEL):
                turn_rows(i + 1, (i + 1) % 4, (i + 1) // 4, i == 0)
                if i == 0:
                    pe.wait_ge(e_lo, EARLY)
                elif i in SPLITS[EARLY:]:
                    pe.wait_ge(w_lo, 2 * (SPLITS.index(i) + 1 - EARLY))
                expert(i, i % 2)
            with pe.Fori(PEEL // 4, LOOPED // 4) as i:
                for q in range(4):
                    turn_rows(4 * i + q + 1, (q + 1) % 4, i + (q + 1) // 4)
                    expert(4 * i + q, q % 2)
            for i in range(LOOPED, SLOT_TILES):
                if i + 1 < SLOT_TILES:
                    turn_rows(i + 1, (i + 1) % 4, (i + 1) // 4)
                expert(i, i % 2)

            def turn_comb(g):
                pe.wait_ge(c_done, g + 1)
                if g >= 2:
                    pe.wait_ge(c_lo, g - 1)
                transpose_tile(comb[:, g % R, :], g % 2).then_inc(c_t, 1)

            def project(g):
                h, k = g % 2, (SLOT_TILES + g) % 2
                pe.wait_ge(ab_read, 24 * B + SLOT_TILES + g + 1)
                nc.tensor.matmul(ab[:, k, :], one_row[:, :], pb_h[:, :], start=True, stop=False)
                nc.tensor.matmul(ab[:, k, :], one_row[:, :], pb_l[:, :], start=False, stop=False)
                pe.wait_ge(c_lo, g + 1)
                for c in range(KC):
                    last = product(ab[:, k, :], st_h[:, h, c, :], st_l[:, h, c, :],
                                   pw_h[:, c, :], pw_l[:, c, :], False, c == KC - 1)
                last.then_inc(ab_full, 1)

            pe.wait_ge(g_lo, SLOT_TILES)
            pe.wait_ge(w_lo, LATE)
            pe.wait_ge(pb_lo, 2)
            turn_comb(0)
            for g in range(G):
                if g + 1 < G:
                    turn_comb(g + 1)
                project(g)

    return None


def kernel(**inputs):
    import numpy as np
    import concourse.bacc as bacc
    from concourse.bass_utils import run_bass_kernel_spmd

    a = {k: np.asarray(v) for k, v in inputs.items()}
    x = a["L0_attn_hidden_states"]
    D = x.shape[-1]
    arrays = {
        "x": x,
        "w_qkv": a["L0_attn_w_qkv"],
        "b_qkv": a["L0_attn_b_qkv"].reshape(3, D // P, P).transpose(2, 0, 1),
        "w_out_t": a["L0_attn_w_out"].T,
        "b_out": a["L0_attn_b_out"],
        "router_w": a["L0_ffn_router_w"],
        "router_b": a["L0_ffn_router_b"],
        "expert_w": a["L0_ffn_expert_w"],
        "expert_b": a["L0_ffn_expert_b"],
        "proj_w": a["L0_ffn_proj_w"],
        "proj_b": a["L0_ffn_proj_b"],
        "norm_w": a["L0_ffn_norm_w"],
    }
    arrays = {f"in_{k}": np.ascontiguousarray(v) for k, v in arrays.items()}
    nc = bacc.Bacc("TRN2", target_bir_lowering=False, num_devices=1)
    args = [nc.dram_tensor(k, v.shape, F32, kind="ExternalInput").ap() for k, v in arrays.items()]
    out = nc.dram_tensor("out", x.shape, F32, kind="ExternalOutput").ap()
    gated_attention_moe(nc, *args, out)
    r = run_bass_kernel_spmd(nc, [arrays], core_ids=[0])
    return r.results[0]["out"]
```
